# Optimizing a Trainium2 kernel written in Bass

```python
import numpy as np
import jax
import jax.numpy as jnp

def _softmax(x, axis=-1):
    return jax.nn.softmax(x, axis=axis)

def _gelu(x):
    return jax.nn.gelu(x, approximate=True)

def _silu(x):
    return jax.nn.silu(x)

def _sigmoid(x):
    return jax.nn.sigmoid(x)

def _layernorm(x, axis=-1, eps=1e-05):
    m = jnp.mean(x, axis=axis, keepdims=True)
    v = jnp.var(x, axis=axis, keepdims=True)
    return (x - m) / jnp.sqrt(v + eps)

def _scatter_add(tgt, idx, src, axis=0):
    return tgt.at[idx].add(src)

def _segment_sum(src, seg, n):
    return jax.ops.segment_sum(src, seg, n)
kernel_name = 'mk_adj_resnorm_d4_adj_r2_f4a031'

def setup_inputs(seed: int=0):
    np.random.seed(seed)
    _w = jnp.asarray

    def _rec_inputs():
        import jax
        import jax.numpy as jnp
        _gk = jax.random.key(seed)
        x = -0.0001117 + 0.9999 * jax.random.normal(jax.random.fold_in(_gk, 1), (16, 512, 256), jnp.float32)
        _a = jax.random.bernoulli(jax.random.fold_in(_gk, 2), 0.03125, (512, 512))
        adj = _a.astype(jnp.int32)
        return (x, adj)
    x, adj = _rec_inputs()

    def _L0_gnn_setup():
        import jax, jax.numpy as jnp
        import numpy as np
        B, N, F, F1 = (512, 75, 256, 128)
        NEG = -1000000000.0
        ALPHA = 0.2
        key = jax.random.key(seed)
        k1, k2, k3, k4 = jax.random.split(key, 4)
        X = jax.random.normal(k1, (B, N, F), dtype=jnp.float32)
        A = jax.random.randint(k2, (N, N), 0, 2, dtype=jnp.int32)
        W = jax.random.normal(k3, (F, F1), dtype=jnp.float32) * (1.0 / np.sqrt(F))
        a = jax.random.normal(k4, (2, F1, 1), dtype=jnp.float32) * (1.0 / np.sqrt(F1))
        return {'X': X, 'A': A, 'W': W, 'a': a}
    _L0_gnn_all = _L0_gnn_setup()
    _L0_gnn_in = {k: v for k, v in _L0_gnn_all.items() if k in ('W', 'a')}
    del _L0_gnn_all

    def _L1_gnn_setup():
        import jax, jax.numpy as jnp
        import numpy as np
        D_MODEL = 256
        NUM_HEADS = 8
        D_HEAD = D_MODEL // NUM_HEADS
        B, N = (4, 1024)
        key = jax.random.key(seed)
        ks = jax.random.split(key, 10)
        s = 1.0 / np.sqrt(D_MODEL)
        inp = {'h': jax.random.normal(ks[0], (B, N, D_MODEL), dtype=jnp.float32), 'adj': jax.random.randint(ks[1], (N, N), 0, 2, dtype=jnp.int32), 'Wq': jax.random.uniform(ks[2], (D_MODEL, D_MODEL), jnp.float32, -s, s), 'bq': jax.random.uniform(ks[3], (D_MODEL,), jnp.float32, -s, s), 'Wk': jax.random.uniform(ks[4], (D_MODEL, D_MODEL), jnp.float32, -s, s), 'bk': jax.random.uniform(ks[5], (D_MODEL,), jnp.float32, -s, s), 'Wv': jax.random.uniform(ks[6], (D_MODEL, D_MODEL), jnp.float32, -s, s), 'bv': jax.random.uniform(ks[7], (D_MODEL,), jnp.float32, -s, s), 'Wo': jax.random.uniform(ks[8], (D_MODEL, D_MODEL), jnp.float32, -s, s), 'bo': jax.random.uniform(ks[9], (D_MODEL,), jnp.float32, -s, s)}
        return inp
    _L1_gnn_all = _L1_gnn_setup()
    _L1_gnn_in = {k: v for k, v in _L1_gnn_all.items() if k in ('Wq', 'bq', 'Wk', 'bk', 'Wv', 'bv', 'Wo', 'bo')}
    del _L1_gnn_all

    def _L2_gnn_setup():
        import jax, jax.numpy as jnp
        import numpy as np
        B, K, DIN, DOUT = (32, 64, 256, 256)
        key = jax.random.key(seed)
        k1, k2, k3, k4 = jax.random.split(key, 4)
        x = jax.random.normal(k1, (B, K, DIN), dtype=jnp.float32)
        adj = jax.random.randint(k2, (K, K), 0, 2, dtype=jnp.int32)
        W = jax.random.normal(k3, (DOUT, 2 * DIN), dtype=jnp.float32) * 0.02
        b = jax.random.normal(k4, (DOUT,), dtype=jnp.float32) * 0.02
        return {'x': x, 'adj': adj, 'W': W, 'b': b}
    _L2_gnn_all = _L2_gnn_setup()
    _L2_gnn_in = {k: v for k, v in _L2_gnn_all.items() if k in ('W', 'b')}
    del _L2_gnn_all

    def _L3_gnn_setup():
        import jax, jax.numpy as jnp
        import numpy as np
        LEAKY_ALPHA = 0.01
        NEG_INF = -1000000000.0
        LN_EPS = 1e-05

        def _gat_heads(x, adj, W, a):
            O = W.shape[-1]
            Wh = jnp.einsum('bnf,hfo->bhno', x, W)
            f1 = jnp.einsum('bhno,ho->bhn', Wh, a[:, :O])
            f2 = jnp.einsum('bhno,ho->bhn', Wh, a[:, O:])
            e = f1[:, :, :, None] + f2[:, :, None, :]
            e = jnp.where(e > 0, e, LEAKY_ALPHA * e)
            e = jnp.where(adj[None, None] > 0, e, NEG_INF)
            attn = jax.nn.softmax(e, axis=-1)
            return jnp.einsum('bhnm,bhmo->bhno', attn, Wh)
        key = jax.random.key(seed)
        ks = jax.random.split(key, 10)
        B, N, F_in, F_hid, H, F_out, D_ff = (8, 1024, 256, 256, 4, 256, 256)
        s = 0.05
        return {'enc_inputs': jax.random.normal(ks[0], (B, N, F_in), jnp.float32), 'adj': jax.random.randint(ks[1], (N, N), 0, 2, jnp.int32), 'W_heads': jax.random.normal(ks[2], (H, F_in, F_hid), jnp.float32) * s, 'a_heads': jax.random.normal(ks[3], (H, 2 * F_hid), jnp.float32) * s, 'W_out': jax.random.normal(ks[4], (H * F_hid, F_out), jnp.float32) * s, 'a_out': jax.random.normal(ks[5], (2 * F_out,), jnp.float32) * s, 'w1': jax.random.normal(ks[6], (F_out, D_ff), jnp.float32) * s, 'b1': jnp.zeros((D_ff,), jnp.float32), 'w2': jax.random.normal(ks[7], (D_ff, F_out), jnp.float32) * s, 'b2': jnp.zeros((F_out,), jnp.float32), 'ln_gamma': jnp.ones((F_out,), jnp.float32), 'ln_beta': jnp.zeros((F_out,), jnp.float32)}
    _L3_gnn_all = _L3_gnn_setup()
    _L3_gnn_in = {k: v for k, v in _L3_gnn_all.items() if k in ('W_heads', 'a_heads', 'W_out', 'a_out', 'w1', 'b1', 'w2', 'b2', 'ln_gamma', 'ln_beta')}
    del _L3_gnn_all
    return {'x': x, 'adj': adj, 'L0_gnn_W': _L0_gnn_in['W'], 'L0_gnn_a': _L0_gnn_in['a'], 'L1_gnn_Wq': _L1_gnn_in['Wq'], 'L1_gnn_bq': _L1_gnn_in['bq'], 'L1_gnn_Wk': _L1_gnn_in['Wk'], 'L1_gnn_bk': _L1_gnn_in['bk'], 'L1_gnn_Wv': _L1_gnn_in['Wv'], 'L1_gnn_bv': _L1_gnn_in['bv'], 'L1_gnn_Wo': _L1_gnn_in['Wo'], 'L1_gnn_bo': _L1_gnn_in['bo'], 'L2_gnn_W': _L2_gnn_in['W'], 'L2_gnn_b': _L2_gnn_in['b'], 'L3_gnn_W_heads': _L3_gnn_in['W_heads'], 'L3_gnn_a_heads': _L3_gnn_in['a_heads'], 'L3_gnn_W_out': _L3_gnn_in['W_out'], 'L3_gnn_a_out': _L3_gnn_in['a_out'], 'L3_gnn_w1': _L3_gnn_in['w1'], 'L3_gnn_b1': _L3_gnn_in['b1'], 'L3_gnn_w2': _L3_gnn_in['w2'], 'L3_gnn_b2': _L3_gnn_in['b2'], 'L3_gnn_ln_gamma': _L3_gnn_in['ln_gamma'], 'L3_gnn_ln_beta': _L3_gnn_in['ln_beta']}

def reference(x, adj, L0_gnn_W, L0_gnn_a, L1_gnn_Wq, L1_gnn_bq, L1_gnn_Wk, L1_gnn_bk, L1_gnn_Wv, L1_gnn_bv, L1_gnn_Wo, L1_gnn_bo, L2_gnn_W, L2_gnn_b, L3_gnn_W_heads, L3_gnn_a_heads, L3_gnn_W_out, L3_gnn_a_out, L3_gnn_w1, L3_gnn_b1, L3_gnn_w2, L3_gnn_b2, L3_gnn_ln_gamma, L3_gnn_ln_beta):
    import jax
    import jax.numpy as jnp

    def _L0_gnn_ref(X, A, W, a):
        import jax, jax.numpy as jnp
        import numpy as np
        B, N, F, F1 = (512, 75, 256, 128)
        NEG = -1000000000.0
        ALPHA = 0.2
        h = jnp.einsum('bnf,fo->bno', X, W)
        att_self = jnp.einsum('bno,od->bnd', h, a[0])
        att_neigh = jnp.einsum('bno,od->bnd', h, a[1])
        e = att_self + jnp.swapaxes(att_neigh, 1, 2)
        e = jax.nn.leaky_relu(e, ALPHA)
        adj = A.astype(h.dtype)
        e = e + NEG * (1.0 - adj)[None, :, :]
        alpha = jax.nn.softmax(e, axis=-1)
        out = jnp.einsum('bij,bjo->bio', alpha, h)
        return jnp.concatenate([out, h], axis=-1)

    def _L1_gnn_ref(h, adj, Wq, bq, Wk, bk, Wv, bv, Wo, bo):
        import jax, jax.numpy as jnp
        import numpy as np
        D_MODEL = 256
        NUM_HEADS = 8
        D_HEAD = D_MODEL // NUM_HEADS
        B, N = (4, 1024)
        b, n, _ = h.shape

        def split_heads(x):
            return x.reshape(b, n, NUM_HEADS, D_HEAD).transpose(0, 2, 1, 3)
        q = split_heads(h @ Wq.T + bq)
        k = split_heads(h @ Wk.T + bk)
        v = split_heads(h @ Wv.T + bv)
        scale = 1.0 / np.sqrt(D_HEAD)
        scores = jnp.einsum('bhqd,bhkd->bhqk', q, k) * scale
        mask = (adj == 0)[None, None, :, :]
        scores = jnp.where(mask, -jnp.inf, scores)
        attn = jax.nn.softmax(scores, axis=-1)
        out = jnp.einsum('bhqk,bhkd->bhqd', attn, v)
        out = out.transpose(0, 2, 1, 3).reshape(b, n, D_MODEL)
        return out @ Wo.T + bo

    def _L2_gnn_ref(x, adj, W, b):
        import jax, jax.numpy as jnp
        import numpy as np
        B, K, DIN, DOUT = (32, 64, 256, 256)
        Din = x.shape[-1]
        Wi, Wj = (W[:, :Din], W[:, Din:])
        mi = jnp.einsum('bkd,od->bko', x, Wi)
        mj = jnp.einsum('bkd,od->bko', x, Wj)
        a = adj.astype(x.dtype)
        deg = a.sum(axis=1)
        out = deg[None, :, None] * (mi + b) + jnp.einsum('ij,bjo->bio', a, mj)
        return out

    def _L3_gnn_ref(enc_inputs, adj, W_heads, a_heads, W_out, a_out, w1, b1, w2, b2, ln_gamma, ln_beta):
        import jax, jax.numpy as jnp
        import numpy as np
        LEAKY_ALPHA = 0.01
        NEG_INF = -1000000000.0
        LN_EPS = 1e-05

        def _gat_heads(x, adj, W, a):
            O = W.shape[-1]
            Wh = jnp.einsum('bnf,hfo->bhno', x, W)
            f1 = jnp.einsum('bhno,ho->bhn', Wh, a[:, :O])
            f2 = jnp.einsum('bhno,ho->bhn', Wh, a[:, O:])
            e = f1[:, :, :, None] + f2[:, :, None, :]
            e = jnp.where(e > 0, e, LEAKY_ALPHA * e)
            e = jnp.where(adj[None, None] > 0, e, NEG_INF)
            attn = jax.nn.softmax(e, axis=-1)
            return jnp.einsum('bhnm,bhmo->bhno', attn, Wh)
        B, N, _ = enc_inputs.shape
        h = jax.nn.elu(_gat_heads(enc_inputs, adj, W_heads, a_heads))
        h = jnp.transpose(h, (0, 2, 1, 3)).reshape(B, N, -1)
        out = _gat_heads(h, adj, W_out[None], a_out[None])[:, 0]
        out = jax.nn.elu(out)
        ffn = jnp.maximum(out @ w1 + b1, 0.0) @ w2 + b2
        y = ffn + out
        mu = jnp.mean(y, axis=-1, keepdims=True)
        var = jnp.var(y, axis=-1, keepdims=True)
        return (y - mu) / jnp.sqrt(var + LN_EPS) * ln_gamma + ln_beta
    x = _layernorm(x + _L0_gnn_ref(x, adj, L0_gnn_W, L0_gnn_a), axis=-1)
    x = _layernorm(x + _L1_gnn_ref(x, adj, L1_gnn_Wq, L1_gnn_bq, L1_gnn_Wk, L1_gnn_bk, L1_gnn_Wv, L1_gnn_bv, L1_gnn_Wo, L1_gnn_bo), axis=-1)
    x = _layernorm(x + _L2_gnn_ref(x, adj, L2_gnn_W, L2_gnn_b), axis=-1)
    x = _layernorm(x + _L3_gnn_ref(x, adj, L3_gnn_W_heads, L3_gnn_a_heads, L3_gnn_W_out, L3_gnn_a_out, L3_gnn_w1, L3_gnn_b1, L3_gnn_w2, L3_gnn_b2, L3_gnn_ln_gamma, L3_gnn_ln_beta), axis=-1)
    return x

_drawn_inputs = setup_inputs


def setup_inputs(seed=0):
    import zlib

    import numpy as np

    out = dict(_drawn_inputs(seed))
    spreads = {'L3_gnn_b1': (0.0, 0.1),
     'L3_gnn_b2': (0.0, 0.1),
     'L3_gnn_ln_gamma': (1.0, 0.2),
     'L3_gnn_ln_beta': (0.0, 0.1)}
    factors = {'L1_gnn_bq': 8.0, 'L1_gnn_bk': 8.0}
    for name, (base, spread) in spreads.items():
        noise = np.random.default_rng([zlib.crc32(name.encode()), seed]).standard_normal(out[name].shape)
        drawn = base * np.exp(spread * noise) if base else spread * noise
        out[name] = jnp.asarray(drawn.astype(out[name].dtype))
    for name, factor in factors.items():
        out[name] = (out[name] * factor).astype(out[name].dtype)
    return out
```

```python
from contextlib import ExitStack

import concourse.bass as bass
from concourse import mybir

P = 128
F32 = mybir.dt.float32
F32R = mybir.dt.float32r
ALU = mybir.AluOpType
ACT = mybir.ActivationFunctionType
AX_X = mybir.AxisListType.X

NO_EDGE = -2.0 ** 37
SLOPE_0, SLOPE_3 = 0.2, 0.01
EPS = 1e-5
START_MAX, START_MIN = -3e38, 3e38


class Signals:

    def __init__(self, new_semaphore, order):
        self.new, self.order, self.seen, self.sems = new_semaphore, order, {}, {}

    def sem(self, name):
        if name not in self.sems:
            self.sems[name] = self.new(name)
        return self.sems[name]

    def raised(self, name, key=0):
        self.seen.setdefault(name, []).append(key)
        return self.sem(name)

    def count(self, name, key, batch):
        order = self.order.get(name) or [key]
        return batch * len(order) + (order.index(key) + 1 if key in order else 1)


def gat_mix_program(nc, x, adj, adj_t, w0, a0, wq_t, bq, wk_t, bk, wv_t, bv, wo_t, bo, w2_t, b2, wh, ah, wout,
                    aout, f1, fb1, f2, fb2, gamma, beta, out, order):
    B, N, F = x.shape
    T = N // P
    KF = F // P
    H0 = w0.shape[1]
    H1, D1 = 8, F // 8
    G1 = H1 * D1 // P
    HG = P // D1
    H3 = wh.shape[0]
    SCALE1 = float(D1) ** -0.5
    assert N == 512 and F == 256 and H0 == 128 and G1 == 2

    with ExitStack() as ctx:
        def sb(name, shape, dt=F32):
            return ctx.enter_context(nc.sbuf_tensor(name, shape, dt))

        def new_semaphore(name):
            return ctx.enter_context(nc.semaphore(name))

        sig = Signals(new_semaphore, order)

        def wait(eng, batch, name, key=0):
            eng.wait_ge(sig.sem(name), sig.count(name, key, batch))

        ident = sb("ident", [P, P])
        neg_half = sb("neg_half", [P, T])
        edge_bias = sb("edge_bias", [P, T, N], mybir.dt.bfloat16)
        adj_t_r = sb("adj_t_r", [P, T, N], F32R)
        degree = sb("degree", [P, T])
        has_edge = sb("has_edge", [P, T])
        w0_sb = sb("w0_sb", [P, KF, H0])
        a0_bc = sb("a0_bc", [P, 2, H0])
        wo_sb = sb("wo_sb", [P, KF, F])
        f2_sb = sb("f2_sb", [P, KF, F])
        bq_c = sb("bq_c", [P, G1])
        bk_c = sb("bk_c", [P, G1])
        fb1_c = sb("fb1_c", [P, KF])
        rows = {n: sb(n + "_bc", [P, F]) for n in ("bv", "bo", "b2", "fb2", "gamma", "beta")}
        ah_bc = sb("ah_bc", [P, H3, 2, F])
        ao_bc = sb("ao_bc", [P, 2, F])
        split = {}
        for n, src, k, m in (("wq", wq_t, KF, F), ("wk", wk_t, KF, F), ("wv", wv_t, KF, F), ("w2", w2_t, KF, 2 * F),
                             ("wh", wh, KF, H3 * F), ("wo3", wout, H3 * KF, F), ("f1", f1, KF, F)):
            split[n] = (src, sb(n + "_hi", [P, k, m], F32R), sb(n + "_lo", [P, k, m], F32R))

        x_in = sb("x_in", [P, T, F])
        xb = sb("xb", [P, T, F])
        yb = sb("yb", [P, T, F])
        xt = sb("xt", [P, KF, N])
        xt_hi = sb("xt_hi", [P, KF, N], F32R)
        xt_lo = sb("xt_lo", [P, KF, N], F32R)
        ht_hi = sb("ht_hi", [P, KF, N], F32R)
        ht_lo = sb("ht_lo", [P, KF, N], F32R)
        h_sb = sb("h_sb", [P, T, F])
        vals = sb("vals", [P, 2, T, F])
        m_hi, m_lo = (m[:].rearrange("p k n -> p (k n)").rearrange("p (t f) -> p t f", f=F) for m in (ht_hi, ht_lo))
        qk_all = sb("qk_all", [P, 4, G1 * N])
        qk = {n: qk_all[:, i, :].bitcast(F32R).rearrange("p (g n) -> p g n", g=G1)
              for i, n in enumerate(("q_hi", "q_lo", "k_hi", "k_lo"))}
        q_st_rest = sb("q_st", [P, H1 - 2 * KF, N], F32R)
        q_st = [ht_hi[:, h, :] if h < KF else ht_lo[:, h - KF, :] if h < 2 * KF else q_st_rest[:, h - 2 * KF, :]
                for h in range(H1)]
        k_st_all = sb("k_st", [P, H1, N], F32R)
        k_st = [k_st_all[:, h, :] for h in range(H1)]
        g_row = sb("g_row", [P, T, N])
        masked = g_row[:, 0:2, :]
        relu_s = qk_all[:, 1, :].rearrange("p (j n) -> p j n", j=2)
        probs = sb("probs", [P, 4, N])
        probs_t = sb("probs_t", [P, 2 * HG, N])
        stage = probs_t[:].rearrange("p a n -> p (a n)")
        o_t = xt
        r_t = h_sb[:].rearrange("p t f -> p (t f)").rearrange("p (g n) -> p g n", g=G1)
        sums = sb("sums", [P, T, H1])
        rden = sb("rden", [P, T, H1])
        neg_max = sb("neg_max", [P, T * H1])
        f_c, g_c, g_max = sb("f_c", [P, T]), sb("g_c", [P, T]), sb("g_max", [P, T])
        z_max, lz_max = sb("z_max", [P, T]), sb("lz_max", [P, T])
        exp_bias, relu_bias = sb("exp_bias", [P, T]), sb("relu_bias", [P, T])
        sums_g, rden_g = sb("sums_g", [P, T]), sb("rden_g", [P, T])
        stats, mv = sb("stats", [P, T, 6]), sb("mv", [P, T, 2])
        var_eps, rstd = sb("var_eps", [P, T]), sb("rstd", [P, T])
        junk = qk_all[:, 0, :].rearrange("p (t f) -> p t f", f=F)
        el = qk_all[:, 2, :].rearrange("p (j n) -> p j n", j=2)
        elm = qk_all[:, 3, :].rearrange("p (j n) -> p j n", j=2)

        banks = [ctx.enter_context(nc.psum_tensor(f"bank{i}", [P, 512], F32)) for i in range(8)]
        mm_list = (["h0", "g0", "q0", "k0", "q1", "k1", "v0", "v1"] + [("s", n) for n in range(T * H1)]
                   + ["r0", "r1", "w0", "w1", "mj0", "mj1", "mi0", "mi1"]
                   + [(n, h) for h in range(H3) for n in ("wh0", "wh1", "g")] + [("g", H3), "f0", "f1", "e0", "e1"])
        tr_list = ([("x", 0, k) for k in range(KF)] + [("p0", t) for t in range(T)] + [("x", 1, k) for k in range(KF)]
                   + [("p1", n) for n in range(T * H1)] + [("x", 2, k) for k in range(KF)] + [("x", 3, k) for k in range(KF)]
                   + [k for h in range(H3) for k in [("p3", h, t) for t in range(T)] + [("x", 4 + h, k) for k in range(KF)]]
                   + [("p3", H3, t) for t in range(T)] + [("x", 4 + H3, k) for k in range(KF)])
        av_list = ["a0", ("o", 0), ("o", 1), ("am", 0), ("am", 1)] + [("a3", h, j) for h in range(H3 + 1) for j in range(2)]
        place = {k: i % 2 for i, k in enumerate(mm_list)} | {k: 2 + i % 2 for i, k in enumerate(tr_list)} \
            | {k: 4 + i % 2 for i, k in enumerate(av_list)} | {("acc", 0): 6, ("acc", 1): 7}
        nth = {}
        for keys in (mm_list, tr_list, av_list, [("acc", 0), ("acc", 1)]):
            for k in keys:
                nth[k] = [j for j in keys if place[j] == place[k]].index(k)
        per_bank = [sum(p == i for p in place.values()) for i in range(8)]
        full = [new_semaphore(f"bank{i}_full") for i in range(8)]
        drained = [new_semaphore(f"bank{i}_drained") for i in range(8)]

        def bank(key):
            return banks[place[key]]

        def wait_drained(pe, b, key):
            pe.wait_ge(drained[place[key]], b * per_bank[place[key]] + nth[key] + 1)

        def wait_full(eng, b, key):
            eng.wait_ge(full[place[key]], b * per_bank[place[key]] + nth[key] + 1)

        def read_out(b, key):
            return drained[place[key]], b * per_bank[place[key]] + nth[key] + 2

        loaded = new_semaphore("loaded")
        x_loaded = new_semaphore("x_loaded")
        stacked = [new_semaphore(f"stacked{g}") for g in range(G1)]
        stored = new_semaphore("stored")
        staged = new_semaphore("staged")
        constants = new_semaphore("constants")
        waits_taken = new_semaphore("waits_taken")
        split_hi = new_semaphore("split_hi")
        ready = new_semaphore("setup_ready")
        SP_STACK = 2 * HG * HG

        def gat_key(kind, idx, t=0):
            if kind == "g":
                return "g0" if idx == 0 else ("g", idx - 1)
            return ("p0", t) if idx == 0 else ("p3", idx - 1, t)

        def gat_vals(idx):
            return 0 if idx == 0 else (idx - 1) % 2

        def gat_slot(idx, t):
            return gat_vals(idx) * T + t

        def wait_weighed(eng, b, n):
            if n % T == T - 1:
                wait_full(eng, b, ("o", n // T))
            else:
                wait(eng, b, "weighed", n)

        def transposed_high(h, high, wait, act, b):
            if 0 < h < H3:
                wait(act, b, "gathered", h - 1)
            elif h == H3:
                for j in range(2):
                    wait_full(act, b, ("acc", j))
            for k in range(KF):
                high(("x", 4 + h, k), ht_hi[:, k, :])

        pieces = []
        for n, (src, hi, _) in split.items():
            k, m = hi.shape[1], hi.shape[2]
            step = max(1, 2048 // m)
            pieces += [(n, a, min(a + step, k)) for a in range(0, k, step)]
        NP_ = len(pieces)
        small_loads = []

        block = ctx.enter_context(nc.Block())

        @block.sync
        def _(sp):
            sp.sem_inc(stored, 16)

            def load(dst, src, **kw):
                sp.dma_start(dst, src, **kw).then_inc(loaded, 16)
                small_loads.append(1)

            load(w0_sb[:], w0.rearrange("(k p) n -> p k n", p=P))
            load(wo_sb[:], wo_t.rearrange("(k p) n -> p k n", p=P))
            load(f2_sb[:], f2.rearrange("(k p) n -> p k n", p=P))
            load(bq_c[:], bq.rearrange("(k p) -> p k", p=P), allow_slow_non_contiguous=True)
            load(bk_c[:], bk.rearrange("(k p) -> p k", p=P), allow_slow_non_contiguous=True)
            load(fb1_c[:], fb1.rearrange("(k p) -> p k", p=P), allow_slow_non_contiguous=True)
            for n, src in (("bv", bv), ("bo", bo), ("b2", b2), ("fb2", fb2), ("gamma", gamma), ("beta", beta)):
                load(rows[n][:], src.partition_broadcast(P))
            for j in range(2):
                load(a0_bc[:, j, :], a0[j].rearrange("n o -> (n o)").partition_broadcast(P))
                load(ao_bc[:, j, :], aout[j * F:(j + 1) * F].partition_broadcast(P))
            for h in range(H3):
                load(ah_bc[:, h].rearrange("p j f -> p (j f)"), ah[h].partition_broadcast(P))
            load(g_row[:].bitcast(mybir.dt.int32), adj.rearrange("(t p) n -> p t n", p=P))
            load(probs[:].bitcast(mybir.dt.int32), adj_t.rearrange("(t p) n -> p t n", p=P))
            sp.dma_start(x_in[:], x[0].rearrange("(t p) f -> p t f", p=P)).then_inc(x_loaded, 16)
            for i, (n, a, z) in enumerate(pieces):
                if i:
                    sp.wait_ge(constants, i)
                src, hi, _ = split[n]
                m = hi.shape[2]
                dst = stage[:, 0:(z - a) * m].rearrange("p (k n) -> p k n", n=m)
                if n == "wh":
                    for k in range(a, z):
                        sp.dma_start(dst[:, k - a, :].rearrange("p (h o) -> p h o", h=H3),
                                     src[:, k * P:(k + 1) * P, :].rearrange("h p o -> p h o")).then_inc(staged, 16)
                else:
                    sp.dma_start(dst, src.rearrange("(k p) n -> p k n", p=P)[:, a:z, :]).then_inc(staged, 16)

            def batch(b, last):
                for g in range(G1):
                    for n, st, parts in (("q", q_st, "hhll"), ("k", k_st, "hlhl")):
                        sp.wait_ge(*read_out(b, f"{n}{g}"))
                        for c, part in enumerate(parts):
                            src = qk[n + ("_hi" if part == "h" else "_lo")]
                            for hh in range(HG):
                                sp.dma_start(st[g * HG + hh][c * D1:(c + 1) * D1, :].bitcast(F32),
                                             src[hh * D1:(hh + 1) * D1, g, :].bitcast(F32)).then_inc(stacked[g], 16)
                    if not last and g == 0:
                        sp.wait_ge(*read_out(b, "a0"))
                        sp.dma_start(x_in[:], x[b + 1].rearrange("(t p) f -> p t f", p=P)).then_inc(x_loaded, 16)
                wait(sp, b, "norm", (4, T - 1))
                sp.dma_start(out[b].rearrange("(t p) f -> p t f", p=P), yb[:]).then_inc(stored, 16)

            with sp.Fori(0, B - 1) as b:
                batch(b, False)
            batch(B - 1, True)
            sp.wait_ge(stored, 16 * B + 16)

        N_LOADS = len(small_loads)
        n_staged = []
        for n, a, z in pieces:
            n_staged.append((n_staged[-1] if n_staged else 0) + 16 * ((z - a) if n == "wh" else 1))

        @block.gpsimd
        def _(pool):
            pool.memset(ident[:], 0.0).then_inc(ready, 1)
            pool.wait_ge(ready, 1)
            pool.affine_select(out=ident[:], in_=ident[:], compare_op=ALU.not_equal, fill=1.0, base=0,
                               pattern=[[-1, P]], channel_multiplier=1).then_inc(ready, 1)
            pool.memset(neg_half[:], -0.5).then_inc(ready, 1)
            pool.wait_ge(ready, 3)
            with pool.Fori(0, B) as b:
                for n in range(5):
                    wait(pool, b, "var", n)
                    if n:
                        wait(pool, b, "norm", (n - 1, T - 1))
                    pool.tensor_tensor(rstd[:], var_eps[:], neg_half[:], ALU.pow).then_inc(sig.raised("rstd", n), 1)

        READY = 3

        @block.tensor
        def _(pe):
            pe.wait_ge(ready, READY)
            pe.wait_ge(constants, NP_ + 4)
            pe.wait_ge(loaded, 16 * N_LOADS)
            for bank_drained in drained:
                pe.sem_inc(bank_drained, 1)

            with pe.Fori(0, B) as b:
                def transpose_x(n, src, wait_tile):
                    for k in range(KF):
                        wait_drained(pe, b, ("x", n, k))
                        for t in range(T):
                            if k == 0 and wait_tile:
                                wait_tile(t)
                            last = pe.transpose(bank(("x", n, k))[:, t * P:(t + 1) * P],
                                                src[:, t, k * P:(k + 1) * P], ident[:])
                        last.then_inc(full[place[("x", n, k)]], 1)

                def product3(dst, lhs, rhs, ks, first=True, final=True, **kw):
                    passes = [(0, 0), (0, 1), (1, 0)]
                    for k in range(ks):
                        for i, (a, z) in enumerate(passes):
                            last = pe.matmul(dst, lhs[a](k), rhs[z](k), start=first and k == 0 and i == 0,
                                             stop=final and k == ks - 1 and i == 2, **kw)
                    return last

                def token_product(keys, w, lo):
                    for j, key in enumerate(keys):
                        wait_drained(pe, b, key)
                        for t in (2 * j, 2 * j + 1):
                            last = product3(bank(key)[:, (t % 2) * F:(t % 2 + 1) * F],
                                            [lambda k, m=m: m[:, k, t * P:(t + 1) * P] for m in (xt_hi, xt_lo)],
                                            [lambda k, m=m: m[:, k, lo:lo + F] for m in split[w][1:]], KF)
                        last.then_inc(full[place[key]], 1)

                def broadcast_g(key, idx):
                    wait_drained(pe, b, key)
                    wait(pe, b, "dots", (idx, T - 1, 1))
                    for t in range(T):
                        last = pe.matmul(bank(key)[:, t * P:(t + 1) * P], g_c[:, t:t + 1].to_broadcast([P, P]),
                                         ident[:], start=True, stop=True)
                    last.then_inc(full[place[key]], 1)

                def transpose_probs(key, name, idx, slot):
                    wait_drained(pe, b, key)
                    wait(pe, b, name, idx)
                    for j in range(T):
                        last = pe.transpose(bank(key)[:, j * P:(j + 1) * P], probs[:, slot, j * P:(j + 1) * P], ident[:])
                    last.then_inc(full[place[key]], 1)

                pe.wait_ge(x_loaded, b * 16 + 16)
                transpose_x(0, x_in, None)
                wait_drained(pe, b, "h0")
                for k in range(KF):
                    pe.wait_ge(*read_out(b, ("x", 0, k)))
                for t in range(T):
                    for k in range(KF):
                        last = pe.matmul(bank("h0")[:, t * P:(t + 1) * P], xt[:, k, t * P:(t + 1) * P], w0_sb[:, k, :],
                                         start=k == 0, stop=k == KF - 1)
                last.then_inc(full[place["h0"]], 1)
                broadcast_g("g0", 0)
                for t in range(T):
                    transpose_probs(("p0", t), "probs_g", (0, t), t)
                wait_drained(pe, b, "a0")
                for t in range(T):
                    pe.wait_ge(*read_out(b, ("p0", t)))
                    for j in range(T):
                        last = pe.matmul(bank("a0")[:, t * P:(t + 1) * P], probs_t[:, t, j * P:(j + 1) * P],
                                         vals[:, 0, j, 0:H0], start=j == 0, stop=j == T - 1)
                last.then_inc(full[place["a0"]], 1)

                transpose_x(1, xb, lambda t: wait(pe, b, "norm", (0, t)))
                for g in range(G1):
                    for n in "qk":
                        key = f"{n}{g}"
                        wait_drained(pe, b, key)
                        if g == 0 and n == "q":
                            for k in range(KF):
                                pe.wait_ge(*read_out(b, ("x", 1, k)))
                        last = product3(bank(key)[:], [lambda k, m=m: m[:, k, g * P:(g + 1) * P] for m in split["w" + n][1:]],
                                        [lambda k, m=m: m[:, k, :] for m in (xt_hi, xt_lo)], KF)
                        last.then_inc(full[place[key]], 1)
                token_product(["v0", "v1"], "wv", 0)

                def scores(n):
                    g, t, hh = n // (T * HG), n // HG % T, n % HG
                    key, h = ("s", n), n // (T * HG) * HG + n % HG
                    if t == 0 and hh == 0:
                        pe.wait_ge(stacked[g], b * (16 * SP_STACK) + 16 * SP_STACK)
                    wait_drained(pe, b, key)
                    pe.matmul(bank(key)[:], q_st[h][:, t * P:(t + 1) * P], k_st[h], start=True, stop=True)\
                      .then_inc(full[place[key]], 1)

                def weigh(n):
                    g, t = n // T, n % T
                    if t == 0:
                        wait_drained(pe, b, ("o", g))
                    if n == 0:
                        for j in range(2):
                            pe.wait_ge(*read_out(b, f"v{j}"))
                    for hh in (HG - 2, HG - 1):
                        pe.wait_ge(*read_out(b, ("p1", n * HG + hh)))
                    for j in range(T):
                        for hh in range(HG):
                            h = g * HG + hh
                            last = pe.matmul(bank(("o", g))[hh * D1:(hh + 1) * D1, t * P:(t + 1) * P],
                                             vals[:, 1, j, h * D1:(h + 1) * D1],
                                             probs_t[:, (n % 2) * HG + hh, j * P:(j + 1) * P],
                                             start=j == 0, stop=j == T - 1)
                    last.then_inc(sig.raised("weighed", n) if t < T - 1 else full[place[("o", g)]], 1)

                LEAD = 2
                for n in range(T * H1 + LEAD):
                    if n < T * H1:
                        scores(n)
                    if n >= LEAD:
                        transpose_probs(("p1", n - LEAD), "probs1", n - LEAD, (n - LEAD) % 4)
                    if n >= LEAD + HG + 1 and (n - LEAD - 1) % HG == 0:
                        weigh((n - LEAD - 1) // HG - 1)
                weigh(T * G1 - 1)
                wait(pe, b, "rden1")
                for g in range(G1):
                    key = f"r{g}"
                    wait_drained(pe, b, key)
                    for t in range(T):
                        for hh in range(HG):
                            last = pe.matmul(bank(key)[hh * D1:(hh + 1) * D1, t * P:(t + 1) * P],
                                             rden[:, t, g * HG + hh:g * HG + hh + 1].to_broadcast([P, D1]), ident[:],
                                             start=True, stop=True)
                    last.then_inc(full[place[key]], 1)
                for j in range(2):
                    key = f"w{j}"
                    wait_drained(pe, b, key)
                    if j == 0:
                        for g in range(G1):
                            pe.wait_ge(*read_out(b, ("o", g)))
                    for t in (2 * j, 2 * j + 1):
                        for k in range(KF):
                            last = pe.matmul(bank(key)[:, (t % 2) * F:(t % 2 + 1) * F], o_t[:, k, t * P:(t + 1) * P],
                                             wo_sb[:, k, :], start=k == 0, stop=k == KF - 1)
                    last.then_inc(full[place[key]], 1)

                transpose_x(2, xb, lambda t: wait(pe, b, "norm", (1, t)))
                for k in range(KF):
                    pe.wait_ge(*read_out(b, ("x", 2, k)))
                token_product(["mj0", "mj1"], "w2", F)
                token_product(["mi0", "mi1"], "w2", 0)
                for j in range(2):
                    pe.wait_ge(*read_out(b, f"mj{j}"))
                for j in range(2):
                    key = ("am", j)
                    wait_drained(pe, b, key)
                    for t in (2 * j, 2 * j + 1):
                        for c in range(T):
                            for m in (m_hi, m_lo):
                                last = pe.matmul(bank(key)[:, (t % 2) * F:(t % 2 + 1) * F], adj_t_r[:, c, t * P:(t + 1) * P],
                                                 m[:, c, :], start=c == 0 and m is m_hi, stop=c == T - 1 and m is m_lo)
                    last.then_inc(full[place[key]], 1)

                transpose_x(3, xb, lambda t: wait(pe, b, "norm", (2, t)))
                for k in range(KF):
                    pe.wait_ge(*read_out(b, ("x", 3, k)))

                def head_values(h):
                    token_product([("wh0", h), ("wh1", h)], "wh", h * F)

                def weigh_head(h):
                    for j in range(2):
                        key = ("a3", h, j)
                        wait_drained(pe, b, key)
                        for t in (2 * j, 2 * j + 1):
                            pe.wait_ge(*read_out(b, ("p3", h, t)))
                            for c in range(T):
                                last = pe.matmul(bank(key)[:, (t % 2) * F:(t % 2 + 1) * F],
                                                 probs_t[:, (h % 2) * T + t, c * P:(c + 1) * P], vals[:, h % 2, c, :],
                                                 start=c == 0, stop=c == T - 1)
                        last.then_inc(full[place[key]], 1)

                def gather_head(h):
                    transpose_x(4 + h, h_sb, lambda t: wait(pe, b, "elu", (h, t // 2)))
                    for k in range(KF):
                        pe.wait_ge(*read_out(b, ("x", 4 + h, k)))
                    if h == H3:
                        return
                    for j in range(2):
                        if h == 0:
                            wait_drained(pe, b, ("acc", j))
                        for t in (2 * j, 2 * j + 1):
                            last = product3(bank(("acc", j))[:, (t % 2) * F:(t % 2 + 1) * F],
                                            [lambda k, m=m: m[:, k, t * P:(t + 1) * P] for m in (ht_hi, ht_lo)],
                                            [lambda k, m=m: m[:, h * KF + k, :] for m in split["wo3"][1:]], KF,
                                            first=h == 0 and t % 2 == 0, final=h == H3 - 1 and t % 2 == 1,
                                            skip_group_check=True)
                        if h == H3 - 1:
                            last.then_inc(full[place[("acc", j)]], 1)
                        elif j == 1:
                            last.then_inc(sig.raised("gathered", h), 1)

                head_values(0)
                broadcast_g(("g", 0), 1)
                for h in range(H3 + 1):
                    if h + 1 < H3:
                        head_values(h + 1)
                    for t in range(T):
                        transpose_probs(("p3", h, t), "probs_g", (1 + h, t), t)
                    if h + 1 < H3:
                        broadcast_g(("g", h + 1), 2 + h)
                    weigh_head(h)
                    gather_head(h)
                    if h == H3 - 1:
                        broadcast_g(("g", H3), 1 + H3)
                for m_ in range(KF):
                    key = f"f{m_}"
                    wait_drained(pe, b, key)
                    last = product3(bank(key)[:], [lambda k, m=m: m[:, k, m_ * P:(m_ + 1) * P] for m in split["f1"][1:]],
                                    [lambda k, m=m: m[:, k, :] for m in (ht_hi, ht_lo)], KF)
                    last.then_inc(full[place[key]], 1)
                for j in range(2):
                    key = f"e{j}"
                    wait_drained(pe, b, key)
                    if j == 0:
                        for m_ in range(KF):
                            pe.wait_ge(*read_out(b, f"f{m_}"))
                    for t in (2 * j, 2 * j + 1):
                        for k in range(KF):
                            last = pe.matmul(bank(key)[:, (t % 2) * F:(t % 2 + 1) * F], xt[:, k, t * P:(t + 1) * P],
                                             f2_sb[:, k, :], start=k == 0, stop=k == KF - 1)
                    last.then_inc(full[place[key]], 1)

        @block.scalar
        def _(act):
            with act.Fori(0, B) as b:
                def drain(key, dst, func=ACT.Copy, **kw):
                    wait_full(act, b, key)
                    act.activation(dst, bank(key)[:], func, **kw).then_inc(drained[place[key]], 1)

                def high(key, dst, func=ACT.Copy, **kw):
                    wait_full(act, b, key)
                    act.activation(dst, bank(key)[:], func, **kw).then_inc(sig.raised("high", key), 1)

                def relu(idx, t, slope):
                    act.wait_ge(*read_out(b, gat_key("g", idx)))
                    wait(act, b, "relu_bias", idx)
                    if t >= 2:
                        wait(act, b, "score", (idx, t - 2))
                    act.activation(relu_s[:, t % 2, :], g_row[:, t, :], ACT.Relu, bias=relu_bias[:, t:t + 1],
                                   scale=1 - slope).then_inc(sig.raised("relu", (idx, t)), 1)

                def exp_g(idx, t):
                    wait(act, b, "score", (idx, t))
                    if idx:
                        wait_full(act, b, gat_key("p", idx - 1, t))
                    act.activation(probs[:, t, :], g_row[:, t, :], ACT.Exp, bias=exp_bias[:, t:t + 1],
                                   accum_out=sums_g[:, t:t + 1]).then_inc(sig.raised("probs_g", (idx, t)), 1)

                def move_probs(idx, t):
                    key = gat_key("p", idx, t)
                    drain(key, probs_t[:, gat_slot(idx, t), :])

                def elu_exp(h, j):
                    wait(act, b, "elm", (h, j))
                    act.activation(elm[:, j, :], elm[:, j, :], ACT.Exp).then_inc(sig.raised("elu_exp", (h, j)), 1)

                for k in range(KF):
                    drain(("x", 0, k), xt[:, k, :])
                wait_full(act, b, "h0")
                act.activation(vals[:, 0, :, 0:H0], bank("h0")[:].rearrange("p (t n) -> p t n", n=H0), ACT.Copy)\
                   .then_inc(drained[place["h0"]], 1)
                relu(0, 0, SLOPE_0)
                relu(0, 1, SLOPE_0)
                for t in range(T):
                    exp_g(0, t)
                    if t + 2 < T:
                        relu(0, t + 2, SLOPE_0)
                    if t % 2:
                        move_probs(0, t - 1)

                for k in range(KF):
                    high(("x", 1, k), xt_hi[:, k, :])
                for g in range(G1):
                    high(f"q{g}", qk["q_hi"][:, g, :], ACT.Identity, bias=bq_c[:, g:g + 1])
                    high(f"k{g}", qk["k_hi"][:, g, :], ACT.Identity, bias=bk_c[:, g:g + 1])

                def exp1(n):
                    act.wait_ge(*read_out(b, ("s", n)))
                    if n >= 4:
                        wait_full(act, b, ("p1", n - 4))
                    h, t = n // (T * HG) * HG + n % HG, n // HG % T
                    act.activation(probs[:, n % 4, :], masked[:, n % 2, :], ACT.Exp, bias=neg_max[:, n:n + 1], scale=-1.0,
                                   accum_out=sums[:, t, h:h + 1]).then_inc(sig.raised("probs1", n), 1)

                for n in range(T * H1 + 2):
                    if n < T * H1:
                        exp1(n)
                    if n >= 2 and n % 2 == 0:
                        if n - 2 >= 2 * HG:
                            wait_weighed(act, b, (n - 2) // HG - 2)
                        drain(("p1", n - 2), probs_t[:, (n - 2) % (2 * HG), :])
                for g in range(G1):
                    drain(f"r{g}", r_t[:, g, :])

                for k in range(KF):
                    high(("x", 2, k), xt_hi[:, k, :])
                for j in range(2):
                    high(f"mj{j}", m_hi[:, 2 * j:2 * j + 2, :].rearrange("p t f -> p (t f)"))

                for k in range(KF):
                    high(("x", 3, k), xt_hi[:, k, :])

                def move_values(h):
                    for j in range(2):
                        key = (f"wh{j}", h) if h < H3 else ("acc", j)
                        if j == 0 and h >= 2:
                            wait_full(act, b, ("a3", h - 2, 1))
                        drain(key, vals[:, h % 2, 2 * j:2 * j + 2, :].rearrange("p t f -> p (t f)"))

                move_values(0)
                for idx in range(1, H3 + 2):
                    h = idx - 1
                    overlapped = 0 < h < H3
                    relu(idx, 0, SLOPE_3)
                    relu(idx, 1, SLOPE_3)
                    exp_g(idx, 0)
                    relu(idx, 2, SLOPE_3)
                    exp_g(idx, 1)
                    if overlapped:
                        elu_exp(h - 1, 0)
                        elu_exp(h - 1, 1)
                    relu(idx, 3, SLOPE_3)
                    exp_g(idx, 2)
                    exp_g(idx, 3)
                    if overlapped:
                        transposed_high(h - 1, high, wait, act, b)
                    move_probs(idx, 0)
                    if h + 1 < H3:
                        move_values(h + 1)
                    move_probs(idx, 2)
                    if h >= H3 - 1:
                        elu_exp(h, 0)
                        elu_exp(h, 1)
                        transposed_high(h, high, wait, act, b)
                        if h == H3 - 1:
                            move_values(H3)
                for m in range(KF):
                    drain(f"f{m}", xt[:, m, :], ACT.Relu, bias=fb1_c[:, m:m + 1])

        @block.vector
        def _(dve):
            dve.wait_ge(loaded, 16 * N_LOADS)
            done = 0
            for i, (n, a, z) in enumerate(pieces):
                _, hi, lo = split[n]
                m = hi.shape[2]
                src = stage[:, 0:(z - a) * m].rearrange("p (k n) -> p k n", n=m)
                dve.wait_ge(staged, n_staged[i])
                dve.tensor_copy(hi[:, a:z, :], src).then_inc(split_hi, 1)
                dve.wait_ge(split_hi, i + 1)
                dve.tensor_tensor(lo[:, a:z, :], src, hi[:, a:z, :].bitcast(F32), ALU.subtract).then_inc(constants, 1)
            adj_i, adj_ti = g_row[:].bitcast(mybir.dt.int32), probs[:].bitcast(mybir.dt.int32)
            dve.tensor_copy(adj_t_r[:], adj_ti).then_inc(constants, 1)
            dve.tensor_scalar(edge_bias[:], adj_i, -NO_EDGE, NO_EDGE, ALU.mult, ALU.add).then_inc(constants, 1)
            dve.tensor_reduce(degree[:], adj_i, AX_X, ALU.add).then_inc(constants, 1)
            dve.wait_ge(constants, NP_ + 3)
            dve.tensor_scalar(has_edge[:], degree[:], 1.0, None, ALU.min).then_inc(constants, 1)
            dve.wait_ge(constants, NP_ + 4)
            dve.wait_ge(ready, READY)

            with dve.Fori(0, B) as b:
                def settled():
                    dve.sem_inc(waits_taken, 1)

                def after(name, key=0):
                    wait(dve, b, name, key)

                def low(key, dst, hi, bias=None):
                    after("high", key)
                    if bias is None:
                        dve.tensor_tensor(dst, bank(key)[:], hi.bitcast(F32), ALU.subtract).then_inc(drained[place[key]], 1)
                    else:
                        dve.scalar_tensor_tensor(dst, bank(key)[:], bias, hi.bitcast(F32), ALU.add, ALU.subtract)\
                           .then_inc(drained[place[key]], 1)

                def norm(n, dst):
                    for t in range(T):
                        dve.bn_stats(stats[:, t, :], yb[:, t, :]).then_inc(sig.raised("stats", (n, t)), 1)
                    for t in range(T):
                        after("stats", (n, t))
                        settled()
                        dve.bn_aggr(mv[:, t, :], stats[:, t, :]).then_inc(sig.raised("mean_var", (n, t)), 1)
                    after("mean_var", (n, T - 1))
                    dve.tensor_scalar(var_eps[:], mv[:, :, 1], EPS, None, ALU.add).then_inc(sig.raised("var", n), 1)
                    after("rstd", n)
                    for t in range(T):
                        dve.tensor_scalar(dst[:, t, :], yb[:, t, :], mv[:, t, 0:1], rstd[:, t:t + 1], ALU.subtract,
                                          ALU.mult).then_inc(sig.raised("norm", (n, t)), 1)

                def row_dots(idx, width, a_of):
                    slot = gat_vals(idx)
                    keys = {0: ["h0"]}.get(idx) or ([(f"wh{j}", idx - 1) for j in range(2)] if idx <= H3 else
                                                    [("acc", j) for j in range(2)])
                    for key in keys:
                        dve.wait_ge(*read_out(b, key))
                    for t in range(T):
                        for j in range(2):
                            if t >= 2:
                                after("dots", (idx, t - 2, j))
                            elif idx:
                                after("dots", (idx - 1, t + 2, j))
                            dve.tensor_tensor_reduce(junk[:, (2 * t + j) % 4, 0:width], vals[:, slot, t, 0:width], a_of(j), 1.0, 0.0,
                                                     ALU.mult, ALU.add, (f_c, g_c)[j][:, t:t + 1])\
                               .then_inc(sig.raised("dots", (idx, t, j)), 1)

                def mask_rows(idx, slope):
                    key = gat_key("g", idx)
                    for t in range(T):
                        if t == 0:
                            wait_full(dve, b, key)
                        if idx:
                            after("probs_g", (idx - 1, t))
                        settled()
                        sem = drained[place[key]] if t == T - 1 else sig.raised("masked_g", (idx, t))
                        dve.tensor_tensor_reduce(g_row[:, t, :], bank(key)[:], edge_bias[:, t, :], 1.0, START_MAX,
                                                 ALU.add, ALU.max, g_max[:, t:t + 1]).then_inc(sem, 1)
                    dve.tensor_scalar(relu_bias[:], f_c[:], 1 - slope, None, ALU.mult).then_inc(sig.raised("relu_bias", idx), 1)
                    dve.wait_ge(*read_out(b, key))
                    dve.tensor_tensor(z_max[:], g_max[:], f_c[:], ALU.add).then_inc(sig.raised("z_max", idx), 1)
                    after("z_max", idx)
                    dve.scalar_tensor_tensor(lz_max[:], z_max[:], slope, z_max[:], ALU.mult, ALU.max)\
                       .then_inc(sig.raised("lz_max", idx), 1)
                    after("lz_max", idx)
                    dve.scalar_tensor_tensor(exp_bias[:], f_c[:], slope, lz_max[:], ALU.mult, ALU.subtract)\
                       .then_inc(sig.raised("exp_bias", idx), 1)

                def score(idx, t, slope):
                    after("relu", (idx, t))
                    dve.scalar_tensor_tensor(g_row[:, t, :], g_row[:, t, :], slope, relu_s[:, t % 2, :], ALU.mult, ALU.add)\
                       .then_inc(sig.raised("score", (idx, t)), 1)

                def move_probs(idx, t):
                    key = gat_key("p", idx, t)
                    wait_full(dve, b, key)
                    dve.tensor_copy(probs_t[:, gat_slot(idx, t), :], bank(key)[:]).then_inc(drained[place[key]], 1)

                def one_over_sums(idx):
                    after("probs_g", (idx, T - 1))
                    dve.reciprocal(rden_g[:], sums_g[:]).then_inc(sig.raised("rden_g", idx), 1)

                def elu_in(h, j):
                    key = ("a3", h, j)
                    wait_full(dve, b, key)
                    after("rden_g", 1 + h)
                    for i in range(2):
                        t = 2 * j + i
                        sem = drained[place[key]] if i else sig.raised("el", (h, j))
                        dve.tensor_scalar(el[:, j, i * F:(i + 1) * F], bank(key)[:, i * F:(i + 1) * F], rden_g[:, t:t + 1],
                                          None, ALU.mult).then_inc(sem, 1)
                    dve.wait_ge(*read_out(b, key))
                    dve.tensor_scalar(elm[:, j, :], el[:, j, :], 0.0, None, ALU.min).then_inc(sig.raised("elm", (h, j)), 1)

                def elu_out(h, j):
                    after("elu_exp", (h, j))
                    dve.scalar_tensor_tensor(h_sb[:, 2 * j:2 * j + 2, :].rearrange("p t f -> p (t f)"), elm[:, j, :], -1.0,
                                             el[:, j, :], ALU.add, ALU.max).then_inc(sig.raised("elu", (h, j)), 1)

                row_dots(0, H0, lambda j: a0_bc[:, j, :])
                mask_rows(0, SLOPE_0)
                for t in range(T):
                    score(0, t, SLOPE_0)
                one_over_sums(0)
                for t in (1, 3):
                    move_probs(0, t)
                dve.wait_ge(stored, b * 16 + 16)
                dve.tensor_tensor(yb[:, :, H0:F], vals[:, 0, :, 0:H0], x_in[:, :, H0:F], ALU.add)\
                   .then_inc(sig.raised("y0", 0), 1)
                wait_full(dve, b, "a0")
                after("rden_g", 0)
                for t in range(T):
                    sem = drained[place["a0"]] if t == T - 1 else sig.raised("y0", 1 + t)
                    dve.scalar_tensor_tensor(yb[:, t, 0:H0], bank("a0")[:, t * P:(t + 1) * P], rden_g[:, t:t + 1],
                                             x_in[:, t, 0:H0], ALU.mult, ALU.add).then_inc(sem, 1)
                dve.wait_ge(*read_out(b, "a0"))
                norm(0, xb)

                for k in range(KF):
                    low(("x", 1, k), xt_lo[:, k, :], xt_hi[:, k, :])
                for g in range(G1):
                    low(f"q{g}", qk["q_lo"][:, g, :], qk["q_hi"][:, g, :], bq_c[:, g:g + 1])
                    low(f"k{g}", qk["k_lo"][:, g, :], qk["k_hi"][:, g, :], bk_c[:, g:g + 1])
                for j in range(2):
                    wait_full(dve, b, f"v{j}")
                    dve.tensor_tensor(vals[:, 1, 2 * j:2 * j + 2, :], bank(f"v{j}")[:].rearrange("p (t f) -> p t f", f=F),
                                      rows["bv"][:].unsqueeze(1).to_broadcast([P, 2, F]), ALU.add)\
                       .then_inc(drained[place[f"v{j}"]], 1)

                def mask_scores(n):
                    key, t = ("s", n), n // HG % T
                    wait_full(dve, b, key)
                    if n >= 2:
                        after("probs1", n - 2)
                    settled()
                    dve.tensor_tensor_reduce(masked[:, n % 2, :], bank(key)[:], edge_bias[:, t, :], -SCALE1, START_MIN,
                                             ALU.add, ALU.min, neg_max[:, n:n + 1]).then_inc(drained[place[key]], 1)

                for n in range(T * H1 + 3):
                    if n < T * H1:
                        mask_scores(n)
                    m = n - 3
                    if m >= 0 and m % 2:
                        if m >= 2 * HG:
                            wait_weighed(dve, b, m // HG - 2)
                        wait_full(dve, b, ("p1", m))
                        dve.tensor_copy(probs_t[:, m % (2 * HG), :], bank(("p1", m))[:]).then_inc(drained[place[("p1", m)]], 1)
                after("probs1", T * H1 - 1)
                dve.tensor_tensor(rden[:], sums[:], has_edge[:].unsqueeze(2).to_broadcast([P, T, H1]), ALU.mult)\
                   .then_inc(sig.raised("sums1"), 1)
                after("sums1")
                dve.reciprocal(rden[:], rden[:]).then_inc(sig.raised("rden1"), 1)
                for g in range(G1):
                    wait_full(dve, b, ("o", g))
                    dve.wait_ge(*read_out(b, f"r{g}"))
                    dve.tensor_tensor(o_t[:, g, :], bank(("o", g))[:], r_t[:, g, :], ALU.mult)\
                       .then_inc(drained[place[("o", g)]], 1)

                def two(m, j):
                    return m[:, 2 * j:2 * j + 2, :]

                def bank2(key):
                    return bank(key)[:].rearrange("p (t f) -> p t f", f=F)

                def row2(n):
                    return rows[n][:].unsqueeze(1).to_broadcast([P, 2, F])

                for j in range(2):
                    key = f"w{j}"
                    wait_full(dve, b, key)
                    dve.tensor_tensor(two(yb, j), bank2(key), row2("bo"), ALU.add).then_inc(drained[place[key]], 1)
                for j in range(2):
                    dve.wait_ge(*read_out(b, f"w{j}"))
                    dve.tensor_tensor(two(yb, j), two(yb, j), two(xb, j), ALU.add).then_inc(sig.raised("y1", j), 1)
                after("y1", 1)
                norm(1, xb)

                for k in range(KF):
                    low(("x", 2, k), xt_lo[:, k, :], xt_hi[:, k, :])
                for j in range(2):
                    low(f"mj{j}", two(m_lo, j).rearrange("p t f -> p (t f)"), two(m_hi, j).rearrange("p t f -> p (t f)"))
                for j in range(2):
                    key = f"mi{j}"
                    wait_full(dve, b, key)
                    dve.tensor_tensor(two(yb, j), bank2(key), row2("b2"), ALU.add).then_inc(drained[place[key]], 1)
                for t in range(T):
                    dve.wait_ge(*read_out(b, f"mi{t // 2}"))
                    dve.scalar_tensor_tensor(yb[:, t, :], yb[:, t, :], degree[:, t:t + 1], xb[:, t, :], ALU.mult, ALU.add)\
                       .then_inc(sig.raised("y2", t), 1)
                after("y2", T - 1)
                for j in range(2):
                    key = ("am", j)
                    wait_full(dve, b, key)
                    dve.tensor_tensor(two(yb, j), bank2(key), two(yb, j), ALU.add).then_inc(drained[place[key]], 1)
                dve.wait_ge(*read_out(b, ("am", 1)))
                dve.wait_ge(*read_out(b, ("am", 0)))
                norm(2, xb)

                for k in range(KF):
                    low(("x", 3, k), xt_lo[:, k, :], xt_hi[:, k, :])

                def low_ht(h):
                    if 0 < h < H3:
                        after("gathered", h - 1)
                    elif h == H3:
                        for j in range(2):
                            wait_full(dve, b, ("acc", j))
                    for k in range(KF):
                        low(("x", 4 + h, k), ht_lo[:, k, :], ht_hi[:, k, :])

                def a_of(idx):
                    return (lambda j: ah_bc[:, idx - 1, j, :]) if idx <= H3 else (lambda j: ao_bc[:, j, :])

                for idx in range(1, H3 + 2):
                    h = idx - 1
                    overlapped = 0 < h < H3
                    row_dots(idx, F, a_of(idx))
                    mask_rows(idx, SLOPE_3)
                    score(idx, 0, SLOPE_3)
                    score(idx, 1, SLOPE_3)
                    if overlapped:
                        elu_in(h - 1, 0)
                        elu_in(h - 1, 1)
                    score(idx, 2, SLOPE_3)
                    if overlapped:
                        elu_out(h - 1, 0)
                    score(idx, 3, SLOPE_3)
                    if overlapped:
                        elu_out(h - 1, 1)
                        low_ht(h - 1)
                    one_over_sums(idx)
                    move_probs(idx, 1)
                    move_probs(idx, 3)
                    if h >= H3 - 1:
                        elu_in(h, 0)
                        elu_in(h, 1)
                        elu_out(h, 0)
                        elu_out(h, 1)
                        low_ht(h)
                for j in range(2):
                    key = f"e{j}"
                    wait_full(dve, b, key)
                    dve.tensor_tensor(two(yb, j), bank2(key), row2("fb2"), ALU.add).then_inc(drained[place[key]], 1)
                for j in range(2):
                    dve.wait_ge(*read_out(b, f"e{j}"))
                    dve.tensor_tensor(two(yb, j), two(yb, j), two(h_sb, j), ALU.add).then_inc(sig.raised("y3", j), 1)
                after("y3", 1)
                norm(3, yb)
                for j in range(2):
                    after("norm", (3, 2 * j + 1))
                    dve.tensor_tensor(two(yb, j), two(yb, j), row2("gamma"), ALU.mult).then_inc(sig.raised("scaled", j), 1)
                for j in range(2):
                    after("scaled", j)
                    dve.tensor_tensor(two(yb, j), two(yb, j), row2("beta"), ALU.add).then_inc(sig.raised("shifted", j), 1)
                for j in range(2):
                    after("shifted", j)
                    dve.tensor_tensor(two(yb, j), two(yb, j), two(xb, j), ALU.add).then_inc(sig.raised("y4", j), 1)
                after("y4", 1)
                norm(4, yb)
    return sig.seen


_INS = ['x', 'adj', 'adj_t', 'L0_gnn_W', 'L0_gnn_a', 'wq_t', 'L1_gnn_bq', 'wk_t', 'L1_gnn_bk', 'wv_t', 'L1_gnn_bv', 'wo_t',
        'L1_gnn_bo', 'w2_t', 'L2_gnn_b', 'L3_gnn_W_heads', 'L3_gnn_a_heads', 'L3_gnn_W_out', 'L3_gnn_a_out', 'L3_gnn_w1',
        'L3_gnn_b1', 'L3_gnn_w2', 'L3_gnn_b2', 'L3_gnn_ln_gamma', 'L3_gnn_ln_beta']


def kernel(**inputs):
    import numpy as _np
    import concourse.bacc as _bacc
    from concourse import mybir as _mybir
    from concourse.bass_utils import run_bass_kernel_spmd as _run

    given = {k: _np.asarray(v) for k, v in inputs.items()}
    for name, src in (("wq_t", "L1_gnn_Wq"), ("wk_t", "L1_gnn_Wk"), ("wv_t", "L1_gnn_Wv"), ("wo_t", "L1_gnn_Wo"),
                      ("adj_t", "adj")):
        given[name] = _np.ascontiguousarray(given[src].T)
    w2 = given["L2_gnn_W"]
    half = w2.shape[1] // 2
    given["w2_t"] = _np.ascontiguousarray(_np.concatenate([w2[:, :half].T, w2[:, half:].T], axis=1))

    def program(order):
        nc = _bacc.Bacc("TRN2", target_bir_lowering=False, num_devices=1)
        arrays, args = {}, []
        for name in _INS:
            a = _np.ascontiguousarray(given[name])
            arrays[f"in_{name}"] = a
            args.append(nc.dram_tensor(f"in_{name}", a.shape, _mybir.dt.from_np(a.dtype), kind="ExternalInput").ap())
        args.append(nc.dram_tensor("out_0", given["x"].shape, _mybir.dt.float32, kind="ExternalOutput").ap())
        return nc, arrays, gat_mix_program(nc, *args, order)

    _, _, order = program({})
    nc, arrays, _ = program(order)
    r = _run(nc, [arrays], core_ids=[0])
    return r.results[0]["out_0"]
```

```python
from contextlib import ExitStack

import concourse.bass as bass
from concourse import mybir

P = 128
F32 = mybir.dt.float32
F32R = mybir.dt.float32r
ALU = mybir.AluOpType
ACT = mybir.ActivationFunctionType
AX_X = mybir.AxisListType.X

NO_EDGE = -2.0 ** 37
SLOPE_0, SLOPE_3 = 0.2, 0.01
EPS = 1e-5
START_MAX, START_MIN = -3e38, 3e38


class Signals:

    def __init__(self, new_semaphore, order):
        self.new, self.order, self.seen, self.sems = new_semaphore, order, {}, {}

    def sem(self, name):
        if name not in self.sems:
            self.sems[name] = self.new(name)
        return self.sems[name]

    def raised(self, name, key=0):
        events = self.seen.setdefault(name, [])
        if key not in events:
            events.append(key)
        return self.sem(name)

    def count(self, name, key, batch):
        order = self.order.get(name) or [key]
        return batch * len(order) + (order.index(key) + 1 if key in order else 1)


def advance(streams, phases):
    at = {name: next(stream, None) for name, stream in streams.items()}
    for name, phase in phases:
        if name in at and at[name] == phase:
            at[name] = next(streams[name], None)
    assert not any(at.values()), at


def merge(front, back):
    out, done = [], [0.0, 0.0]
    lists = [list(front.items()), list(back.items())]
    total = [sum(front.values()), sum(back.values())]
    while lists[0] or lists[1]:
        k = 0 if not lists[1] or (lists[0] and done[0] / total[0] <= done[1] / total[1]) else 1
        phase, weight = lists[k].pop(0)
        done[k] += weight
        out.append(("front back".split()[k], phase))
    last = ("front", list(front)[-1])
    out.remove(last)
    return out + [last]


def gat_mix_program(nc, x, adj, adj_t, w0, a0, wq_t, bq, wk_t, bk, wv_t, bv, wo_t, bo, w2_t, b2, wh, ah, wout,
                    aout, f1, fb1, f2, fb2, gamma, beta, out, order):
    B, N, F = x.shape
    T = N // P
    KF = F // P
    H0 = w0.shape[1]
    H1, D1 = 8, F // 8
    G1 = H1 * D1 // P
    HG = P // D1
    H3 = wh.shape[0]
    SCALE1 = float(D1) ** -0.5
    assert N == 512 and F == 256 and H0 == 128 and G1 == 2

    with ExitStack() as ctx:
        def sb(name, shape, dt=F32):
            return ctx.enter_context(nc.sbuf_tensor(name, shape, dt))

        def new_semaphore(name):
            return ctx.enter_context(nc.semaphore(name))

        sig = Signals(new_semaphore, order)

        def raise_of(batch, name, key=0):
            return sig.sem(name), sig.count(name, key, batch)

        ident = sb("ident", [P, P])
        neg_half = sb("neg_half", [P, T])
        edge_bias = sb("edge_bias", [P, T, N], mybir.dt.bfloat16)
        adj_t_r = sb("adj_t_r", [P, T, N], F32R)
        degree = sb("degree", [P, T])
        has_edge = sb("has_edge", [P, T])
        w0_sb = sb("w0_sb", [P, KF, H0])
        a0_bc = sb("a0_bc", [P, 2, H0])
        wo_sb = sb("wo_sb", [P, KF, F])
        wo3_sb = sb("wo3_sb", [P, H3 * KF, F])
        f1_sb = sb("f1_sb", [P, KF, F])
        f2_sb = sb("f2_sb", [P, KF, F])
        bq_c = sb("bq_c", [P, G1])
        bk_c = sb("bk_c", [P, G1])
        fb1_c = sb("fb1_c", [P, KF])
        rows = {n: sb(n + "_bc", [P, F]) for n in ("bv", "bo", "b2", "fb2", "gamma", "beta")}
        ah_bc = sb("ah_bc", [P, H3, 2, F])
        ao_bc = sb("ao_bc", [P, 2, F])
        split = {}
        for n, src, k, m in (("wq", wq_t, KF, F), ("wk", wk_t, KF, F), ("wv", wv_t, KF, F), ("w2", w2_t, KF, 2 * F),
                             ("wh", wh, KF, H3 * F)):
            split[n] = (src, sb(n + "_hi", [P, k, m], F32R), sb(n + "_lo", [P, k, m], F32R))

        sel = {n: (sb("sel_" + n, [P, HG, len(blocks) * D1], F32R), blocks, low_from)
               for n, blocks, low_from in (("q", (1, 1, 0, 0, 1, 1), 2), ("k", (1, 0, 1, 0, 1), 1))}

        xa = sb("xa", [P, T, F])
        xt = sb("xt", [P, KF, N])
        o_t = xt
        xt_hi, xt_lo = sb("xt_hi", [P, KF, N], F32R), sb("xt_lo", [P, KF, N], F32R)
        vals_a = sb("vals_a", [P, T, F])
        q_st = sb("q_st", [P, HG, N], F32R)
        k_st = sb("k_st", [P, HG, N], F32R)
        qk = {n: k_st[:, i, :] for i, n in enumerate(("q_hi", "q_lo", "k_hi", "k_lo"))}
        m_hi, m_lo = (m[:, 0:2, :].rearrange("p a n -> p (a n)").rearrange("p (t f) -> p t f", f=F) for m in (q_st, k_st))
        xb = sb("xb", [P, T, F])
        xu_hi, xu_lo = sb("xu_hi", [P, KF, N], F32R), sb("xu_lo", [P, KF, N], F32R)
        vals_b = sb("vals_b", [P, 2, T, F])
        el = sb("el", [P, 2, 2 * F])
        h_sb = sb("h_sb", [P, T, F])
        ht = sb("ht", [P, KF, N])

        def two(m, j):
            return m[:, 2 * j:2 * j + 2, :]

        def flat2(m, j):
            return two(m, j).rearrange("p t f -> p (t f)")

        g_row = {s: sb("g_row_" + s, [P, T, N]) for s in "ab"}
        masked = g_row["a"]
        probs = {s: sb("probs_" + s, [P, T, N]) for s in "ab"}
        probs_t = {s: sb("probs_t_" + s, [P, T, N]) for s in "ab"}
        fs_t = g_row["b"][:].rearrange("p t n -> p (t n)")[:, 0:KF * N].rearrange("p (k n) -> p k n", n=N)
        stage = probs_t["a"][:].rearrange("p a n -> p (a n)")
        sums = sb("sums", [P, T, H1])
        rden = sb("rden", [P, T, H1])
        neg_max = sb("neg_max", [P, T * H1])
        names = ("f_c", "g_c", "g_max", "z_max", "lz_max", "exp_bias", "relu_bias", "sums_g", "rden_g", "var_eps", "rstd")
        row = {s: {n: sb(n + "_" + s, [P, T]) for n in names} for s in "ab"}
        stats = {s: sb("stats_" + s, [P, T, 6]) for s in "ab"}
        mv = {s: sb("mv_" + s, [P, T, 2]) for s in "ab"}

        banks = [ctx.enter_context(nc.psum_tensor(f"bank{i}", [P, 512], F32)) for i in range(8)]
        UNITS = T * HG
        LEAD = 2

        front_list = [("x", 0, k) for k in range(KF)] + ["h0", ("g", 0)] + [("p", 0, t) for t in range(T)] + ["a0"]
        front_list += [("x", 1, k) for k in range(KF)] + ["q0", "k0", "v0", "v1"]
        for g in range(G1):
            if g:
                front_list += [f"q{g}", f"k{g}"]
            front_list += [("stack", g, n, hh) for n in "qk" for hh in range(HG)]
            for n in range(UNITS + LEAD + 1):
                if n < UNITS:
                    front_list.append(("s", g, n))
                if n >= LEAD + HG and (n - LEAD) % HG == 0:
                    front_list.append(("o", g, (n - LEAD) // HG - 1))
                if LEAD <= n < UNITS + LEAD:
                    front_list.append(("p1", g, n - LEAD))
            front_list.remove(("o", g, T - 1))
            front_list += [("o", g, T - 1), f"r{g}"]
        front_list += ["w0", "w1"] + [("x", 2, k) for k in range(KF)] + ["mj0", "mj1", "mi0", "mi1", ("am", 0), ("am", 1)]
        back_list = [("x", 3, k) for k in range(KF)] + [("wh0", 0), ("wh1", 0), ("g", 1)]
        for h in range(H3 + 1):
            back_list += [("p", 1 + h, t) for t in range(T)]
            if h + 1 < H3:
                back_list += [("wh0", h + 1), ("wh1", h + 1), ("g", 2 + h)]
            back_list += [("a3", h, j) for j in range(2)] + [("x", 4 + h, k) for k in range(KF)]
            if h == H3 - 1:
                back_list.append(("g", 1 + H3))
        back_list += ["f0", "f1", "e0", "e1"]
        place = {k: i % 3 for i, k in enumerate(front_list)} | {k: 3 + i % 3 for i, k in enumerate(back_list)} \
            | {("acc", 0): 6, ("acc", 1): 7}
        nth = {}
        for keys in (front_list, back_list, [("acc", 0), ("acc", 1)]):
            assert len(set(keys)) == len(keys)
            for k in keys:
                nth[k] = [j for j in keys if place[j] == place[k]].index(k)
        per_bank = [sum(p == i for p in place.values()) for i in range(8)]
        full = [new_semaphore(f"bank{i}_full") for i in range(8)]
        drained = [new_semaphore(f"bank{i}_drained") for i in range(8)]

        def bank(key):
            return banks[place[key]]

        def filled(key):
            return full[place[key]]

        def emptied(key):
            return drained[place[key]]

        def free(b, key, read=()):
            counts = {}
            for k, n in [(key, nth[key] + 1)] + [(k, nth[k] + 2) for k in read]:
                counts[place[k]] = max(n, counts.get(place[k], 0))
            return [(drained[i], b * per_bank[i] + n) for i, n in counts.items()]

        def product_of(b, key):
            return full[place[key]], b * per_bank[place[key]] + (nth[key] + 1)

        def moved(b, key):
            return drained[place[key]], b * per_bank[place[key]] + (nth[key] + 2)

        front = {"x0": 1, "h0": 2, "g0": 2, "score0": 3, "p0": 2, "a0": 4, "stats0": 2, "norm0": 2, "x1": 2, "q0": 3, "v": 3}
        for g in range(G1):
            if g:
                front[f"q{g}"] = 4
            front["stack", g] = 4
            for n in range(UNITS + LEAD):
                front["unit", g, n] = 1.5
            front["o", g] = 1
            front["r", g] = 1.5
        front |= {"w": 3, "stats1": 2, "norm1": 2, "x2": 2, "mj": 3, "mi": 3, "am": 4, "stats2": 2, "norm2": 2}
        back = {"x3": 2, ("wh", 0): 4, ("g3", 0): 2, ("score3", 0): 3}
        for h in range(H3 + 1):
            back["p3", h] = 2
            if h + 1 < H3:
                back["wh", h + 1] = 4
                back["g3", h + 1] = 2
            back["a3", h] = 5
            if h + 1 < H3:
                back["score3", h + 1] = 2
            back["elu", h] = 3
            back["ht", h] = 2
            if h < H3:
                back["acc", h] = 3
            if h == H3 - 1:
                back["values", H3] = 2
                back["g3", H3] = 2
                back["score3", H3] = 4
        back |= {"f": 3, "e": 3, "stats3": 2, "norm3": 4, "stats4": 2, "norm4": 2}

        def both(front_stream, back_stream, fori):
            advance({"front": front_stream(0)}, [("front", p) for p in front])
            with fori(0, B - 1) as b:
                advance({"front": front_stream(b + 1), "back": back_stream(b)}, merge(front, back))
            advance({"back": back_stream(B - 1)}, [("back", p) for p in back])

        def leaky_of(idx):
            if idx == 0:
                return "a", SLOPE_0, vals_a[:, :, 0:H0], lambda j: a0_bc[:, j, :]
            return "b", SLOPE_3, vals_b[:, (idx - 1) % 2], \
                (lambda j: ah_bc[:, idx - 1, j, :]) if idx <= H3 else (lambda j: ao_bc[:, j, :])

        loaded = new_semaphore("loaded")
        x_loaded = new_semaphore("x_loaded")
        stored = new_semaphore("stored")
        staged = new_semaphore("staged")
        constants = new_semaphore("constants")
        waits_taken = new_semaphore("waits_taken")
        sp_waits_taken = new_semaphore("sp_waits_taken")
        split_hi = new_semaphore("split_hi")
        ready = new_semaphore("setup_ready")
        READY = 3

        pieces = []
        for n, (src, hi, _) in split.items():
            k, m = hi.shape[1], hi.shape[2]
            step = max(1, T * N // m)
            pieces += [(n, a, min(a + step, k)) for a in range(0, k, step)]
        NP_ = len(pieces)
        N_CONST = 4 + sum(len(blocks) for _, blocks, _ in sel.values())
        small_loads = []

        block = ctx.enter_context(nc.Block())

        @block.sync
        def _(sp):
            sp.sem_inc(stored, 16)

            def load(dst, src, **kw):
                sp.dma_start(dst, src, **kw).then_inc(loaded, 16)
                small_loads.append(1)

            sp.dma_start(xa[:], x[0].rearrange("(t p) f -> p t f", p=P)).then_inc(x_loaded, 16)
            load(g_row["b"][:].bitcast(mybir.dt.int32), adj.rearrange("(t p) n -> p t n", p=P))
            load(probs["b"][:].bitcast(mybir.dt.int32), adj_t.rearrange("(t p) n -> p t n", p=P))
            load(w0_sb[:], w0.rearrange("(k p) n -> p k n", p=P))
            load(wo_sb[:], wo_t.rearrange("(k p) n -> p k n", p=P))
            load(wo3_sb[:], wout.rearrange("(k p) n -> p k n", p=P))
            load(f1_sb[:], f1.rearrange("(k p) n -> p k n", p=P))
            load(f2_sb[:], f2.rearrange("(k p) n -> p k n", p=P))
            load(bq_c[:], bq.rearrange("(k p) -> p k", p=P), allow_slow_non_contiguous=True)
            load(bk_c[:], bk.rearrange("(k p) -> p k", p=P), allow_slow_non_contiguous=True)
            load(fb1_c[:], fb1.rearrange("(k p) -> p k", p=P), allow_slow_non_contiguous=True)
            for n, src in (("bv", bv), ("bo", bo), ("b2", b2), ("fb2", fb2), ("gamma", gamma), ("beta", beta)):
                load(rows[n][:], src.partition_broadcast(P))
            for j in range(2):
                load(a0_bc[:, j, :], a0[j].rearrange("n o -> (n o)").partition_broadcast(P))
                load(ao_bc[:, j, :], aout[j * F:(j + 1) * F].partition_broadcast(P))
            for h in range(H3):
                load(ah_bc[:, h].rearrange("p j f -> p (j f)"), ah[h].partition_broadcast(P))
            for i, (n, a, z) in enumerate(pieces):
                if i:
                    sp.wait_ge(constants, i)
                src, hi, _ = split[n]
                m = hi.shape[2]
                dst = stage[:, 0:(z - a) * m].rearrange("p (k n) -> p k n", n=m)
                if n == "wh":
                    for k in range(a, z):
                        sp.dma_start(dst[:, k - a, :].rearrange("p (h o) -> p h o", h=H3),
                                     src[:, k * P:(k + 1) * P, :].rearrange("h p o -> p h o")).then_inc(staged, 16)
                else:
                    sp.dma_start(dst, src.rearrange("(k p) n -> p k n", p=P)[:, a:z, :]).then_inc(staged, 16)

            def store(b):
                sp.wait_ge(*raise_of(b, "norm_b", (4, T - 1)))
                sp.sem_inc(sp_waits_taken, 1)
                sp.dma_start(out[b].rearrange("(t p) f -> p t f", p=P), h_sb[:]).then_inc(stored, 16)

            def next_x(b):
                sp.wait_ge(*raise_of(b, "y2", T - 1))
                sp.sem_inc(sp_waits_taken, 1)
                sp.dma_start(xa[:], x[b + 1].rearrange("(t p) f -> p t f", p=P)).then_inc(x_loaded, 16)

            next_x(0)
            with sp.Fori(0, B - 2) as b:
                store(b)
                next_x(b + 1)
            store(B - 2)
            store(B - 1)
            sp.wait_ge(stored, 16 * B + 16)

        N_LOADS = len(small_loads)
        n_staged = []
        for n, a, z in pieces:
            n_staged.append((n_staged[-1] if n_staged else 0) + 16 * ((z - a) if n == "wh" else 1))

        @block.gpsimd
        def _(pool):
            pool.memset(ident[:], 0.0).then_inc(ready, 1)
            pool.wait_ge(ready, 1)
            pool.affine_select(out=ident[:], in_=ident[:], compare_op=ALU.not_equal, fill=1.0, base=0,
                               pattern=[[-1, P]], channel_multiplier=1).then_inc(ready, 1)
            pool.memset(neg_half[:], -0.5).then_inc(ready, 1)
            pool.wait_ge(ready, READY)

            def root(b, n):
                s = "a" if n < 3 else "b"
                pool.wait_ge(*raise_of(b, "var_" + s, n))
                pool.tensor_tensor(row[s]["rstd"][:], row[s]["var_eps"][:], neg_half[:], ALU.pow)\
                    .then_inc(sig.raised("rstd_" + s, n), 1)

            def front_stream(b):
                for n in range(3):
                    yield f"stats{n}"
                    root(b, n)

            def back_stream(b):
                for n in (3, 4):
                    yield f"stats{n}"
                    root(b, n)

            both(front_stream, back_stream, pool.Fori)

        @block.tensor
        def _(pe):
            pe.wait_ge(ready, READY)
            pe.wait_ge(constants, NP_ + N_CONST)
            pe.wait_ge(loaded, 16 * N_LOADS)
            for bank_drained in drained:
                pe.sem_inc(bank_drained, 1)

            def transpose_x(b, n, src, wait_tile):
                for k in range(KF):
                    for count in free(b, ("x", n, k)):
                        pe.wait_ge(*count)
                    for t in range(T):
                        if k == 0 and wait_tile:
                            wait_tile(t)
                        last = pe.transpose(bank(("x", n, k))[:, t * P:(t + 1) * P], src[:, t, k * P:(k + 1) * P], ident[:])
                    last.then_inc(filled(("x", n, k)), 1)

            def product3(dst, lhs, rhs, ks):
                for k in range(ks):
                    for i, (a, z) in enumerate([(0, 0), (0, 1), (1, 0)]):
                        last = pe.matmul(dst, lhs[a](k), rhs[z](k), start=k == 0 and i == 0,
                                         stop=k == ks - 1 and i == 2)
                return last

            def token_product(b, keys, xs, w, lo, read=()):
                for j, key in enumerate(keys):
                    for count in free(b, key, () if j else read):
                        pe.wait_ge(*count)
                    for t in (2 * j, 2 * j + 1):
                        last = product3(bank(key)[:, (t % 2) * F:(t % 2 + 1) * F],
                                        [lambda k, m=m: m[:, k, t * P:(t + 1) * P] for m in xs],
                                        [lambda k, m=m: m[:, k, lo:lo + F] for m in split[w][1:]], KF)
                    last.then_inc(filled(key), 1)

            def broadcast_g(b, idx):
                s, key = leaky_of(idx)[0], ("g", idx)
                for count in free(b, key):
                    pe.wait_ge(*count)
                pe.wait_ge(*raise_of(b, "dots_" + s, (idx, T - 1, 1)))
                for t in range(T):
                    last = pe.matmul(bank(key)[:, t * P:(t + 1) * P], row[s]["g_c"][:, t:t + 1].to_broadcast([P, P]), ident[:],
                                     start=True, stop=True)
                last.then_inc(filled(key), 1)

            def transpose_probs(b, key, src, name, event):
                for count in free(b, key):
                    pe.wait_ge(*count)
                pe.wait_ge(*raise_of(b, name, event))
                for j in range(T):
                    last = pe.transpose(bank(key)[:, j * P:(j + 1) * P], src[:, j * P:(j + 1) * P], ident[:])
                last.then_inc(filled(key), 1)

            def qk_product(b, g):
                for n in "qk":
                    key = f"{n}{g}"
                    for count in free(b, key, [("x", 1, k) for k in range(KF)] if key == "q0" else ()):
                        pe.wait_ge(*count)
                    last = product3(bank(key)[:], [lambda k, m=m: m[:, k, g * P:(g + 1) * P] for m in split["w" + n][1:]],
                                    [lambda k, m=m: m[:, k, :] for m in (xt_hi, xt_lo)], KF)
                    last.then_inc(filled(key), 1)

            def stack(b, g):
                for n in "qk":
                    for hh in range(HG):
                        key, (ones, _, low_from) = ("stack", g, n, hh), sel[n]
                        for count in free(b, key, [f"{n}{g}"]):
                            pe.wait_ge(*count)
                        pe.matmul(bank(key)[:], ones[:, hh, 0:P], qk[n + "_hi"], start=True, stop=False)
                        pe.matmul(bank(key)[:], ones[:, hh, low_from * D1:low_from * D1 + P], qk[n + "_lo"], start=False,
                                  stop=True).then_inc(filled(key), 1)

            def scores(b, g, n):
                t, hh, key = n // HG, n % HG, ("s", g, n)
                for count in free(b, key, [("stack", g, m, i) for m in "qk" for i in range(HG)] if n == 0 else ()):
                    pe.wait_ge(*count)
                pe.matmul(bank(key)[:], q_st[:, hh, t * P:(t + 1) * P], k_st[:, hh, :], start=True, stop=True)\
                  .then_inc(filled(key), 1)

            def weigh(b, g, t):
                key = ("o", g, t)
                for count in free(b, key, ["v0", "v1"] + [("p1", g, t * HG + hh) for hh in range(HG)]):
                    pe.wait_ge(*count)
                for j in range(T):
                    for hh in range(HG):
                        h = g * HG + hh
                        last = pe.matmul(bank(key)[hh * D1:(hh + 1) * D1, 0:P], vals_a[:, j, h * D1:(h + 1) * D1],
                                         probs_t["a"][:, hh, j * P:(j + 1) * P], start=j == 0, stop=j == T - 1)
                last.then_inc(filled(key), 1)

            def front_stream(b):
                yield "x0"
                pe.wait_ge(x_loaded, b * 16 + 16)
                transpose_x(b, 0, xa, None)
                yield "h0"
                for count in free(b, "h0", [("x", 0, k) for k in range(KF)]):
                    pe.wait_ge(*count)
                for t in range(T):
                    for k in range(KF):
                        last = pe.matmul(bank("h0")[:, t * P:(t + 1) * P], xt[:, k, t * P:(t + 1) * P], w0_sb[:, k, :],
                                         start=k == 0, stop=k == KF - 1)
                last.then_inc(filled("h0"), 1)
                yield "g0"
                broadcast_g(b, 0)
                yield "p0"
                for t in range(T):
                    transpose_probs(b, ("p", 0, t), probs["a"][:, t, :], "probs_g_a", (0, t))
                yield "a0"
                for count in free(b, "a0", [("p", 0, t) for t in range(T)]):
                    pe.wait_ge(*count)
                for t in range(T):
                    for j in range(T):
                        last = pe.matmul(bank("a0")[:, t * P:(t + 1) * P], probs_t["a"][:, t, j * P:(j + 1) * P],
                                         vals_a[:, j, 0:H0], start=j == 0, stop=j == T - 1)
                last.then_inc(filled("a0"), 1)

                yield "x1"
                transpose_x(b, 1, xa, lambda t: pe.wait_ge(*raise_of(b, "norm_a", (0, t))))
                yield "q0"
                qk_product(b, 0)
                yield "v"
                token_product(b, ["v0", "v1"], (xt_hi, xt_lo), "wv", 0)
                for g in range(G1):
                    if g:
                        yield f"q{g}"
                        qk_product(b, g)
                    yield "stack", g
                    stack(b, g)
                    for n in range(UNITS + LEAD):
                        yield "unit", g, n
                        if n < UNITS:
                            scores(b, g, n)
                        if n >= LEAD + HG and (n - LEAD) % HG == 0:
                            weigh(b, g, (n - LEAD) // HG - 1)
                        if n >= LEAD:
                            transpose_probs(b, ("p1", g, n - LEAD), probs["a"][:, (n - LEAD) % T, :], "probs1", (g, n - LEAD))
                    yield "o", g
                    weigh(b, g, T - 1)
                    yield "r", g
                    key = f"r{g}"
                    for count in free(b, key):
                        pe.wait_ge(*count)
                    pe.wait_ge(*raise_of(b, "rden1", g))
                    for t in range(T):
                        for hh in range(HG):
                            last = pe.matmul(bank(key)[hh * D1:(hh + 1) * D1, t * P:(t + 1) * P],
                                             rden[:, t, g * HG + hh:g * HG + hh + 1].to_broadcast([P, D1]), ident[:],
                                             start=True, stop=True)
                    last.then_inc(filled(key), 1)
                yield "w"
                for j in range(2):
                    key = f"w{j}"
                    for count in free(b, key, [f"r{g}" for g in range(G1)]):
                        pe.wait_ge(*count)
                    for t in (2 * j, 2 * j + 1):
                        for k in range(KF):
                            last = pe.matmul(bank(key)[:, (t % 2) * F:(t % 2 + 1) * F], o_t[:, k, t * P:(t + 1) * P],
                                             wo_sb[:, k, :], start=k == 0, stop=k == KF - 1)
                    last.then_inc(filled(key), 1)

                yield "x2"
                transpose_x(b, 2, xa, lambda t: pe.wait_ge(*raise_of(b, "norm_a", (1, t))))
                yield "mj"
                token_product(b, ["mj0", "mj1"], (xt_hi, xt_lo), "w2", F, [("x", 2, k) for k in range(KF)])
                yield "mi"
                token_product(b, ["mi0", "mi1"], (xt_hi, xt_lo), "w2", 0)
                yield "am"
                for j in range(2):
                    key = ("am", j)
                    for count in free(b, key, ["mj0", "mj1"]):
                        pe.wait_ge(*count)
                    for t in (2 * j, 2 * j + 1):
                        for c in range(T):
                            for m in (m_hi, m_lo):
                                last = pe.matmul(bank(key)[:, (t % 2) * F:(t % 2 + 1) * F], adj_t_r[:, c, t * P:(t + 1) * P],
                                                 m[:, c, :], start=c == 0 and m is m_hi, stop=c == T - 1 and m is m_lo)
                    last.then_inc(filled(key), 1)

            def back_stream(b):
                def head_values(h):
                    token_product(b, [("wh0", h), ("wh1", h)], (xu_hi, xu_lo), "wh", h * F,
                                  () if h else [("x", 3, k) for k in range(KF)])

                yield "x3"
                transpose_x(b, 3, xb, lambda t: pe.wait_ge(*raise_of(b, "norm_a", (2, t))))
                yield "wh", 0
                head_values(0)
                yield "g3", 0
                broadcast_g(b, 1)
                for h in range(H3 + 1):
                    yield "p3", h
                    for t in range(T):
                        transpose_probs(b, ("p", 1 + h, t), probs["b"][:, t, :], "probs_g_b", (1 + h, t))
                    if h + 1 < H3:
                        yield "wh", h + 1
                        head_values(h + 1)
                        yield "g3", h + 1
                        broadcast_g(b, 2 + h)
                    yield "a3", h
                    for j in range(2):
                        key = ("a3", h, j)
                        for count in free(b, key, [("p", 1 + h, t) for t in (2 * j, 2 * j + 1)]):
                            pe.wait_ge(*count)
                        for t in (2 * j, 2 * j + 1):
                            for c in range(T):
                                last = pe.matmul(bank(key)[:, (t % 2) * F:(t % 2 + 1) * F],
                                                 probs_t["b"][:, t, c * P:(c + 1) * P], vals_b[:, h % 2, c, :],
                                                 start=c == 0, stop=c == T - 1)
                        last.then_inc(filled(key), 1)
                    yield "ht", h
                    transpose_x(b, 4 + h, h_sb, lambda t: pe.wait_ge(*raise_of(b, "elu", (h, t // 2))))
                    if h < H3:
                        yield "acc", h
                        for j in range(2):
                            if h == 0:
                                for count in free(b, ("acc", j), [("x", 4 + h, k) for k in range(KF)]):
                                    pe.wait_ge(*count)
                            elif j == 0:
                                for k in range(KF):
                                    pe.wait_ge(*moved(b, ("x", 4 + h, k)))
                            for t in (2 * j, 2 * j + 1):
                                for k in range(KF):
                                    last = pe.matmul(bank(("acc", j))[:, (t % 2) * F:(t % 2 + 1) * F],
                                                     ht[:, k, t * P:(t + 1) * P], wo3_sb[:, h * KF + k, :],
                                                     start=h == 0 and t % 2 == 0 and k == 0,
                                                     stop=h == H3 - 1 and t % 2 == 1 and k == KF - 1,
                                                     skip_group_check=True)
                            if h == H3 - 1:
                                last.then_inc(filled(("acc", j)), 1)
                            elif j == 1:
                                last.then_inc(sig.raised("gathered", h), 1)
                    if h == H3 - 1:
                        yield "g3", H3
                        broadcast_g(b, 1 + H3)
                yield "f"
                for m_ in range(KF):
                    key = f"f{m_}"
                    for count in free(b, key, [("x", 4 + H3, k) for k in range(KF)]):
                        pe.wait_ge(*count)
                    for k in range(KF):
                        last = pe.matmul(bank(key)[:], f1_sb[:, k, m_ * P:(m_ + 1) * P], ht[:, k, :], start=k == 0,
                                         stop=k == KF - 1)
                    last.then_inc(filled(key), 1)
                yield "e"
                for j in range(2):
                    key = f"e{j}"
                    for count in free(b, key, [f"f{m_}" for m_ in range(KF)]):
                        pe.wait_ge(*count)
                    for t in (2 * j, 2 * j + 1):
                        for k in range(KF):
                            last = pe.matmul(bank(key)[:, (t % 2) * F:(t % 2 + 1) * F], fs_t[:, k, t * P:(t + 1) * P],
                                             f2_sb[:, k, :], start=k == 0, stop=k == KF - 1)
                    last.then_inc(filled(key), 1)

            both(front_stream, back_stream, pe.Fori)

        @block.scalar
        def _(act):
            act.wait_ge(constants, NP_ + N_CONST)
            act.wait_ge(loaded, 16 * N_LOADS)

            def drain(b, key, dst, func=ACT.Copy, src=None, **kw):
                act.wait_ge(*product_of(b, key))
                act.activation(dst, bank(key)[:] if src is None else src, func, **kw).then_inc(emptied(key), 1)

            def high(b, key, dst, func=ACT.Copy, **kw):
                act.wait_ge(*product_of(b, key))
                act.activation(dst, bank(key)[:], func, **kw).then_inc(sig.raised("high", key), 1)

            def relus(b, idx):
                s, slope, _, _ = leaky_of(idx)
                act.wait_ge(*moved(b, ("g", idx)))
                act.wait_ge(*raise_of(b, "relu_bias_" + s, idx))
                for t in range(T):
                    if idx > 1:
                        act.wait_ge(*product_of(b, ("p", idx - 1, t)))
                    act.activation(probs[s][:, t, :], g_row[s][:, t, :], ACT.Relu, bias=row[s]["relu_bias"][:, t:t + 1],
                                   scale=1 - slope).then_inc(sig.raised("relu_" + s, (idx, t)), 1)

            def exps(b, idx):
                s = leaky_of(idx)[0]
                for t in range(T):
                    act.wait_ge(*raise_of(b, "score_" + s, (idx, t)))
                    act.activation(probs[s][:, t, :], g_row[s][:, t, :], ACT.Exp, bias=row[s]["exp_bias"][:, t:t + 1],
                                   accum_out=row[s]["sums_g"][:, t:t + 1]).then_inc(sig.raised("probs_g_" + s, (idx, t)), 1)


            def exp1(b, g, n):
                t, h = n // HG, g * HG + n % HG
                act.wait_ge(*moved(b, ("s", g, n)))
                if n >= T:
                    act.wait_ge(*product_of(b, ("p1", g, n - T)))
                elif g:
                    act.wait_ge(*product_of(b, ("p1", g - 1, n + UNITS - T)))
                act.activation(probs["a"][:, n % T, :], masked[:, n % T, :], ACT.Exp,
                               bias=neg_max[:, g * UNITS + n:g * UNITS + n + 1], scale=-1.0,
                               accum_out=sums[:, t, h:h + 1]).then_inc(sig.raised("probs1", (g, n)), 1)

            def front_stream(b):
                yield "x0"
                for k in range(KF):
                    drain(b, ("x", 0, k), xt[:, k, :])
                yield "h0"
                if not isinstance(b, int):
                    act.wait_ge(*raise_of(b - 1, "norm_a", (2, T - 1)))
                drain(b, "h0", vals_a[:, :, 0:H0], src=bank("h0")[:].rearrange("p (t n) -> p t n", n=H0))
                yield "g0"
                relus(b, 0)
                yield "score0"
                exps(b, 0)
                yield "p0"
                for t in range(T):
                    drain(b, ("p", 0, t), probs_t["a"][:, t, :])
                yield "x1"
                for k in range(KF):
                    high(b, ("x", 1, k), xt_hi[:, k, :])
                yield "q0"
                high(b, "q0", qk["q_hi"], ACT.Identity, bias=bq_c[:, 0:1])
                high(b, "k0", qk["k_hi"], ACT.Identity, bias=bk_c[:, 0:1])
                for g in range(G1):
                    if g:
                        yield f"q{g}"
                        act.wait_ge(*product_of(b, ("s", g - 1, UNITS - 1)))
                        high(b, f"q{g}", qk["q_hi"], ACT.Identity, bias=bq_c[:, g:g + 1])
                        high(b, f"k{g}", qk["k_hi"], ACT.Identity, bias=bk_c[:, g:g + 1])
                    yield "stack", g
                    for hh in range(HG):
                        drain(b, ("stack", g, "q", hh), q_st[:, hh, :])
                    for n in range(UNITS + LEAD):
                        yield "unit", g, n
                        if n < UNITS:
                            exp1(b, g, n)
                        m = n - LEAD
                        if m >= 0:
                            if m >= HG and m % HG == 0:
                                t = m // HG - 1
                                drain(b, ("o", g, t), o_t[:, g, t * P:(t + 1) * P], src=bank(("o", g, t))[:, 0:P])
                            elif m == 0 and g:
                                act.wait_ge(*product_of(b, ("o", g - 1, T - 1)))
                            drain(b, ("p1", g, m), probs_t["a"][:, m % HG, :])
                    yield "o", g
                    drain(b, ("o", g, T - 1), o_t[:, g, (T - 1) * P:], src=bank(("o", g, T - 1))[:, 0:P])
                yield "x2"
                for k in range(KF):
                    high(b, ("x", 2, k), xt_hi[:, k, :])
                yield "mj"
                for j in range(2):
                    high(b, f"mj{j}", flat2(m_hi, j))

            def back_stream(b):
                def move_values(h):
                    for j in range(2):
                        key = (f"wh{j}", h) if h < H3 else ("acc", j)
                        if j == 0 and h >= 2:
                            act.wait_ge(*product_of(b, ("a3", h - 2, 1)))
                        drain(b, key, flat2(vals_b[:, h % 2], j))

                yield "x3"
                for k in range(KF):
                    high(b, ("x", 3, k), xu_hi[:, k, :])
                yield "wh", 0
                move_values(0)
                yield "g3", 0
                relus(b, 1)
                yield "score3", 0
                exps(b, 1)
                for h in range(H3 + 1):
                    yield "p3", h
                    for t in range(T):
                        if h and t == 0:
                            act.wait_ge(*product_of(b, ("a3", h - 1, 1)))
                        drain(b, ("p", 1 + h, t), probs_t["b"][:, t, :])
                    if h + 1 < H3:
                        yield "wh", h + 1
                        move_values(h + 1)
                        yield "g3", h + 1
                        relus(b, 2 + h)
                        yield "score3", h + 1
                        exps(b, 2 + h)
                    yield "elu", h
                    for j in range(2):
                        act.wait_ge(*raise_of(b, "elm", (h, j)))
                        act.activation(flat2(h_sb, j), flat2(h_sb, j), ACT.Exp).then_inc(sig.raised("elu_exp", (h, j)), 1)
                    yield "ht", h
                    if 0 < h < H3:
                        act.wait_ge(*raise_of(b, "gathered", h - 1))
                    elif h == H3:
                        for j in range(2):
                            act.wait_ge(*product_of(b, ("acc", j)))
                    for k in range(KF):
                        drain(b, ("x", 4 + h, k), ht[:, k, :])
                    if h == H3 - 1:
                        yield "values", H3
                        move_values(H3)
                        yield "g3", H3
                        relus(b, 1 + H3)
                        yield "score3", H3
                        exps(b, 1 + H3)
                yield "f"
                for m in range(KF):
                    drain(b, f"f{m}", fs_t[:, m, :], ACT.Relu, bias=fb1_c[:, m:m + 1])

            both(front_stream, back_stream, act.Fori)

        @block.vector
        def _(dve):
            dve.wait_ge(loaded, 16 * N_LOADS)
            for i, (n, a, z) in enumerate(pieces):
                _, hi, lo = split[n]
                m = hi.shape[2]
                src = stage[:, 0:(z - a) * m].rearrange("p (k n) -> p k n", n=m)
                dve.wait_ge(staged, n_staged[i])
                dve.tensor_copy(hi[:, a:z, :], src).then_inc(split_hi, 1)
                dve.wait_ge(split_hi, i + 1)
                dve.tensor_tensor(lo[:, a:z, :], src, hi[:, a:z, :].bitcast(F32), ALU.subtract).then_inc(constants, 1)
            adj_i, adj_ti = (m["b"][:].bitcast(mybir.dt.int32) for m in (g_row, probs))
            dve.tensor_copy(adj_t_r[:], adj_ti).then_inc(constants, 1)
            dve.tensor_scalar(edge_bias[:], adj_i, -NO_EDGE, NO_EDGE, ALU.mult, ALU.add).then_inc(constants, 1)
            dve.tensor_reduce(degree[:], adj_i, AX_X, ALU.add).then_inc(constants, 1)
            dve.wait_ge(ready, READY)
            for ones, blocks, _ in sel.values():
                for c, one in enumerate(blocks):
                    dve.tensor_scalar(ones[:, :, c * D1:(c + 1) * D1], ident[:].rearrange("p (h d) -> p h d", d=D1), float(one),
                                      None, ALU.mult).then_inc(constants, 1)
            dve.wait_ge(constants, NP_ + N_CONST - 1)
            dve.tensor_scalar(has_edge[:], degree[:], 1.0, None, ALU.min).then_inc(constants, 1)
            dve.wait_ge(constants, NP_ + N_CONST)

            def settled():
                dve.sem_inc(waits_taken, 1)

            def bank2(key):
                return bank(key)[:].rearrange("p (t f) -> p t f", f=F)

            def row2(n):
                return rows[n][:].unsqueeze(1).to_broadcast([P, 2, F])

            def low(b, key, dst, hi, bias=None):
                dve.wait_ge(*raise_of(b, "high", key))
                if bias is None:
                    dve.tensor_tensor(dst, bank(key)[:], hi.bitcast(F32), ALU.subtract).then_inc(emptied(key), 1)
                else:
                    dve.scalar_tensor_tensor(dst, bank(key)[:], bias, hi.bitcast(F32), ALU.add, ALU.subtract)\
                       .then_inc(emptied(key), 1)

            def norm_stats(b, n, s, src):
                for t in range(T):
                    dve.bn_stats(stats[s][:, t, :], src[:, t, :]).then_inc(sig.raised("stats_" + s, (n, t)), 1)
                for t in range(T):
                    dve.wait_ge(*raise_of(b, "stats_" + s, (n, t)))
                    settled()
                    dve.bn_aggr(mv[s][:, t, :], stats[s][:, t, :]).then_inc(sig.raised("mean_var_" + s, (n, t)), 1)
                dve.wait_ge(*raise_of(b, "mean_var_" + s, (n, T - 1)))
                dve.tensor_scalar(row[s]["var_eps"][:], mv[s][:, :, 1], EPS, None, ALU.add).then_inc(sig.raised("var_" + s, n), 1)

            def norm(b, n, s, src, dst):
                dve.wait_ge(*raise_of(b, "rstd_" + s, n))
                for t in range(T):
                    dve.tensor_scalar(dst[:, t, :], src[:, t, :], mv[s][:, t, 0:1], row[s]["rstd"][:, t:t + 1], ALU.subtract,
                                      ALU.mult).then_inc(sig.raised("norm_" + s, (n, t)), 1)

            def row_dots(b, idx):
                s, _, vals, a_of = leaky_of(idx)
                width = vals.shape[-1]
                for key in ["h0"] if idx == 0 else [(f"wh{j}", idx - 1) for j in range(2)] if idx <= H3 else \
                        [("acc", j) for j in range(2)]:
                    dve.wait_ge(*moved(b, key))
                for t in range(T):
                    for j in range(2):
                        if idx > 1 and j == 0:
                            dve.wait_ge(*raise_of(b, "probs_g_" + s, (idx - 1, t)))
                        dve.tensor_tensor_reduce(g_row[s][:, t, j * width:(j + 1) * width], vals[:, t, :], a_of(j), 1.0, 0.0,
                                                 ALU.mult, ALU.add, row[s]["fg"[j] + "_c"][:, t:t + 1])\
                           .then_inc(sig.raised("dots_" + s, (idx, t, j)), 1)

            def mask_rows(b, idx):
                s, slope, _, _ = leaky_of(idx)
                key, r = ("g", idx), row[s]
                dve.wait_ge(*raise_of(b, "dots_" + s, (idx, T - 1, 1)))
                dve.tensor_scalar(r["relu_bias"][:], r["f_c"][:], 1 - slope, None, ALU.mult)\
                   .then_inc(sig.raised("relu_bias_" + s, idx), 1)
                for t in range(T):
                    if t == 0:
                        dve.wait_ge(*product_of(b, key))
                        settled()
                    sem = emptied(key) if t == T - 1 else sig.raised("masked_g_" + s, (idx, t))
                    dve.tensor_tensor_reduce(g_row[s][:, t, :], bank(key)[:], edge_bias[:, t, :], 1.0, START_MAX,
                                             ALU.add, ALU.max, r["g_max"][:, t:t + 1]).then_inc(sem, 1)
                dve.wait_ge(*moved(b, key))
                dve.tensor_tensor(r["z_max"][:], r["g_max"][:], r["f_c"][:], ALU.add).then_inc(sig.raised("z_max_" + s, idx), 1)
                dve.wait_ge(*raise_of(b, "z_max_" + s, idx))
                dve.scalar_tensor_tensor(r["lz_max"][:], r["z_max"][:], slope, r["z_max"][:], ALU.mult, ALU.max)\
                   .then_inc(sig.raised("lz_max_" + s, idx), 1)
                dve.wait_ge(*raise_of(b, "lz_max_" + s, idx))
                dve.scalar_tensor_tensor(r["exp_bias"][:], r["f_c"][:], slope, r["lz_max"][:], ALU.mult, ALU.subtract)\
                   .then_inc(sig.raised("exp_bias_" + s, idx), 1)

            def score_rows(b, idx):
                s, slope, _, _ = leaky_of(idx)
                for t in range(T):
                    dve.wait_ge(*raise_of(b, "relu_" + s, (idx, t)))
                    if t == 0:
                        dve.wait_ge(*raise_of(b, "exp_bias_" + s, idx))
                    dve.scalar_tensor_tensor(g_row[s][:, t, :], g_row[s][:, t, :], slope, probs[s][:, t, :], ALU.mult, ALU.add)\
                       .then_inc(sig.raised("score_" + s, (idx, t)), 1)

            def one_over_sums(b, idx):
                s = leaky_of(idx)[0]
                dve.wait_ge(*raise_of(b, "probs_g_" + s, (idx, T - 1)))
                dve.reciprocal(row[s]["rden_g"][:], row[s]["sums_g"][:]).then_inc(sig.raised("rden_g_" + s, idx), 1)

            def front_stream(b):
                yield "h0"
                row_dots(b, 0)
                yield "g0"
                mask_rows(b, 0)
                yield "score0"
                score_rows(b, 0)
                yield "p0"
                dve.tensor_tensor(xa[:, :, H0:F], vals_a[:, :, 0:H0], xa[:, :, H0:F], ALU.add)\
                   .then_inc(sig.raised("y0", 0), 1)
                yield "a0"
                one_over_sums(b, 0)
                dve.wait_ge(*product_of(b, "a0"))
                dve.wait_ge(*raise_of(b, "rden_g_a", 0))
                for t in range(T):
                    sem = emptied("a0") if t == T - 1 else sig.raised("y0", 1 + t)
                    dve.scalar_tensor_tensor(xa[:, t, 0:H0], bank("a0")[:, t * P:(t + 1) * P], row["a"]["rden_g"][:, t:t + 1],
                                             xa[:, t, 0:H0], ALU.mult, ALU.add).then_inc(sem, 1)
                yield "stats0"
                dve.wait_ge(*moved(b, "a0"))
                norm_stats(b, 0, "a", xa)
                yield "norm0"
                norm(b, 0, "a", xa, xa)

                yield "x1"
                for k in range(KF):
                    low(b, ("x", 1, k), xt_lo[:, k, :], xt_hi[:, k, :])
                yield "q0"
                low(b, "q0", qk["q_lo"], qk["q_hi"], bq_c[:, 0:1])
                low(b, "k0", qk["k_lo"], qk["k_hi"], bk_c[:, 0:1])
                yield "v"
                for j in range(2):
                    dve.wait_ge(*product_of(b, f"v{j}"))
                    dve.tensor_tensor(two(vals_a, j), bank2(f"v{j}"), row2("bv"), ALU.add).then_inc(emptied(f"v{j}"), 1)
                for g in range(G1):
                    if g:
                        yield f"q{g}"
                        low(b, f"q{g}", qk["q_lo"], qk["q_hi"], bq_c[:, g:g + 1])
                        low(b, f"k{g}", qk["k_lo"], qk["k_hi"], bk_c[:, g:g + 1])
                    yield "stack", g
                    for hh in range(HG):
                        key = ("stack", g, "k", hh)
                        dve.wait_ge(*product_of(b, ("stack", g, "k", HG - 1) if hh >= 2 else key))
                        dve.tensor_copy(k_st[:, hh, :], bank(key)[:]).then_inc(emptied(key), 1)
                    for n in range(UNITS + LEAD):
                        yield "unit", g, n
                        if n < UNITS:
                            key = ("s", g, n)
                            dve.wait_ge(*product_of(b, key))
                            if n >= T or g:
                                before = (g, n - T) if n >= T else (g - 1, n + UNITS - T)
                                dve.wait_ge(*raise_of(b, "probs1", before))
                            settled()
                            dve.tensor_tensor_reduce(masked[:, n % T, :], bank(key)[:], edge_bias[:, n // HG, :], -SCALE1,
                                                     START_MIN, ALU.add, ALU.min,
                                                     neg_max[:, g * UNITS + n:g * UNITS + n + 1]).then_inc(emptied(key), 1)
                    yield "o", g
                    sums_of, rden_of = (m[:, :, g * HG:(g + 1) * HG] for m in (sums, rden))
                    dve.wait_ge(*raise_of(b, "probs1", (g, UNITS - 1)))
                    dve.tensor_tensor(rden_of, sums_of, has_edge[:].unsqueeze(2).to_broadcast([P, T, HG]), ALU.mult)\
                       .then_inc(sig.raised("sums1", g), 1)
                    dve.wait_ge(*raise_of(b, "sums1", g))
                    dve.reciprocal(rden_of, rden_of).then_inc(sig.raised("rden1", g), 1)
                    yield "r", g
                    dve.wait_ge(*product_of(b, f"r{g}"))
                    for bank_i in range(3):
                        keys = [("o", g, t) for t in range(T) if place["o", g, t] == bank_i != place[f"r{g}"]]
                        if keys:
                            dve.wait_ge(*moved(b, keys[-1]))
                    dve.tensor_tensor(o_t[:, g, :], bank(f"r{g}")[:], o_t[:, g, :], ALU.mult).then_inc(emptied(f"r{g}"), 1)
                yield "w"
                for j in range(2):
                    key = f"w{j}"
                    dve.wait_ge(*product_of(b, key))
                    dve.tensor_tensor(two(xa, j), bank2(key), two(xa, j), ALU.add).then_inc(emptied(key), 1)
                for j in range(2):
                    dve.wait_ge(*moved(b, f"w{j}"))
                    dve.tensor_tensor(two(xa, j), two(xa, j), row2("bo"), ALU.add).then_inc(sig.raised("y1", j), 1)
                yield "stats1"
                dve.wait_ge(*raise_of(b, "y1", 1))
                norm_stats(b, 1, "a", xa)
                yield "norm1"
                norm(b, 1, "a", xa, xa)

                yield "x2"
                for k in range(KF):
                    low(b, ("x", 2, k), xt_lo[:, k, :], xt_hi[:, k, :])
                yield "mj"
                for j in range(2):
                    low(b, f"mj{j}", flat2(m_lo, j), flat2(m_hi, j))
                yield "mi"
                for j in range(2):
                    key = f"mi{j}"
                    dve.wait_ge(*product_of(b, key))
                    dve.tensor_tensor(two(vals_a, j), bank2(key), row2("b2"), ALU.add).then_inc(emptied(key), 1)
                for t in range(T):
                    dve.wait_ge(*moved(b, f"mi{t // 2}"))
                    dve.scalar_tensor_tensor(vals_a[:, t, :], vals_a[:, t, :], degree[:, t:t + 1], xa[:, t, :], ALU.mult,
                                             ALU.add).then_inc(sig.raised("y2", t), 1)
                yield "am"
                dve.wait_ge(*raise_of(b, "y2", T - 1))
                for j in range(2):
                    key = ("am", j)
                    dve.wait_ge(*product_of(b, key))
                    dve.tensor_tensor(two(vals_a, j), bank2(key), two(vals_a, j), ALU.add).then_inc(emptied(key), 1)
                yield "stats2"
                for j in range(2):
                    dve.wait_ge(*moved(b, ("am", j)))
                norm_stats(b, 2, "a", vals_a)
                yield "norm2"
                if not isinstance(b, int):
                    dve.wait_ge(*raise_of(b - 1, "y4", 1))
                norm(b, 2, "a", vals_a, xb)

            def back_stream(b):
                yield "x3"
                for k in range(KF):
                    low(b, ("x", 3, k), xu_lo[:, k, :], xu_hi[:, k, :])
                yield "wh", 0
                row_dots(b, 1)
                yield "g3", 0
                mask_rows(b, 1)
                yield "score3", 0
                score_rows(b, 1)
                for h in range(H3 + 1):
                    if h + 1 < H3:
                        yield "wh", h + 1
                        row_dots(b, 2 + h)
                        yield "g3", h + 1
                        mask_rows(b, 2 + h)
                    yield "a3", h
                    one_over_sums(b, 1 + h)
                    if h == 0:
                        dve.wait_ge(stored, b * 16 + 16)
                    for j in range(2):
                        key = ("a3", h, j)
                        dve.wait_ge(*product_of(b, key))
                        dve.wait_ge(*raise_of(b, "rden_g_b", 1 + h))
                        for i in range(2):
                            t = 2 * j + i
                            sem = emptied(key) if i else sig.raised("el", (h, j))
                            dve.tensor_scalar(el[:, j, i * F:(i + 1) * F], bank(key)[:, i * F:(i + 1) * F],
                                              row["b"]["rden_g"][:, t:t + 1], None, ALU.mult).then_inc(sem, 1)
                        dve.wait_ge(*moved(b, key))
                        if h:
                            for k in range(KF):
                                dve.wait_ge(*product_of(b, ("x", 3 + h, k)))
                        dve.tensor_scalar(flat2(h_sb, j), el[:, j, :], 0.0, None, ALU.min).then_inc(sig.raised("elm", (h, j)), 1)
                    if h + 1 < H3:
                        yield "score3", h + 1
                        score_rows(b, 2 + h)
                    yield "elu", h
                    for j in range(2):
                        dve.wait_ge(*raise_of(b, "elu_exp", (h, j)))
                        dve.scalar_tensor_tensor(flat2(h_sb, j), flat2(h_sb, j), -1.0, el[:, j, :], ALU.add, ALU.max)\
                           .then_inc(sig.raised("elu", (h, j)), 1)
                    if h == H3 - 1:
                        yield "values", H3
                        row_dots(b, 1 + H3)
                        yield "g3", H3
                        mask_rows(b, 1 + H3)
                        yield "score3", H3
                        score_rows(b, 1 + H3)
                yield "e"
                for j in range(2):
                    key = f"e{j}"
                    dve.wait_ge(*product_of(b, key))
                    dve.tensor_tensor(two(h_sb, j), bank2(key), two(h_sb, j), ALU.add).then_inc(emptied(key), 1)
                for j in range(2):
                    dve.wait_ge(*moved(b, f"e{j}"))
                    dve.tensor_tensor(two(h_sb, j), two(h_sb, j), row2("fb2"), ALU.add).then_inc(sig.raised("y3", j), 1)
                yield "stats3"
                dve.wait_ge(*raise_of(b, "y3", 1))
                norm_stats(b, 3, "b", h_sb)
                yield "norm3"
                norm(b, 3, "b", h_sb, h_sb)
                for j in range(2):
                    dve.wait_ge(*raise_of(b, "norm_b", (3, 2 * j + 1)))
                    dve.tensor_tensor(two(h_sb, j), two(h_sb, j), row2("gamma"), ALU.mult).then_inc(sig.raised("scaled", j), 1)
                for j in range(2):
                    dve.wait_ge(*raise_of(b, "scaled", j))
                    dve.tensor_tensor(two(h_sb, j), two(h_sb, j), row2("beta"), ALU.add).then_inc(sig.raised("shifted", j), 1)
                for j in range(2):
                    dve.wait_ge(*raise_of(b, "shifted", j))
                    dve.tensor_tensor(two(h_sb, j), two(h_sb, j), two(xb, j), ALU.add).then_inc(sig.raised("y4", j), 1)
                yield "stats4"
                dve.wait_ge(*raise_of(b, "y4", 1))
                norm_stats(b, 4, "b", h_sb)
                yield "norm4"
                norm(b, 4, "b", h_sb, h_sb)

            both(front_stream, back_stream, dve.Fori)
    return sig.seen


_INS = ['x', 'adj', 'adj_t', 'L0_gnn_W', 'L0_gnn_a', 'wq_t', 'L1_gnn_bq', 'wk_t', 'L1_gnn_bk', 'wv_t', 'L1_gnn_bv', 'wo_t',
        'L1_gnn_bo', 'w2_t', 'L2_gnn_b', 'L3_gnn_W_heads', 'L3_gnn_a_heads', 'L3_gnn_W_out', 'L3_gnn_a_out', 'L3_gnn_w1',
        'L3_gnn_b1', 'L3_gnn_w2', 'L3_gnn_b2', 'L3_gnn_ln_gamma', 'L3_gnn_ln_beta']


def kernel(**inputs):
    import numpy as _np
    import concourse.bacc as _bacc
    from concourse import mybir as _mybir
    from concourse.bass_utils import run_bass_kernel_spmd as _run

    given = {k: _np.asarray(v) for k, v in inputs.items()}
    for name, src in (("wq_t", "L1_gnn_Wq"), ("wk_t", "L1_gnn_Wk"), ("wv_t", "L1_gnn_Wv"), ("wo_t", "L1_gnn_Wo"),
                      ("adj_t", "adj")):
        given[name] = _np.ascontiguousarray(given[src].T)
    w2 = given["L2_gnn_W"]
    half = w2.shape[1] // 2
    given["w2_t"] = _np.ascontiguousarray(_np.concatenate([w2[:, :half].T, w2[:, half:].T], axis=1))

    def program(order):
        nc = _bacc.Bacc("TRN2", target_bir_lowering=False, num_devices=1)
        arrays, args = {}, []
        for name in _INS:
            a = _np.ascontiguousarray(given[name])
            arrays[f"in_{name}"] = a
            args.append(nc.dram_tensor(f"in_{name}", a.shape, _mybir.dt.from_np(a.dtype), kind="ExternalInput").ap())
        args.append(nc.dram_tensor("out_0", given["x"].shape, _mybir.dt.float32, kind="ExternalOutput").ap())
        return nc, arrays, gat_mix_program(nc, *args, order)

    _, _, order = program({})
    nc, arrays, _ = program(order)
    r = _run(nc, [arrays], core_ids=[0])
    return r.results[0]["out_0"]
```

```python
from contextlib import ExitStack

import concourse.bass as bass
from concourse import mybir

P = 128
F32 = mybir.dt.float32
F32R = mybir.dt.float32r
ALU = mybir.AluOpType
ACT = mybir.ActivationFunctionType
AX_X = mybir.AxisListType.X

NO_EDGE = -2.0 ** 37
SLOPE_0, SLOPE_3 = 0.2, 0.01
EPS = 1e-5
START_MAX, START_MIN = -3e38, 3e38


class Signals:

    def __init__(self, new_semaphore, order):
        self.new, self.order, self.seen, self.sems = new_semaphore, order, {}, {}

    def sem(self, name):
        if name not in self.sems:
            self.sems[name] = self.new(name)
        return self.sems[name]

    def raised(self, name, key=0):
        events = self.seen.setdefault(name, [])
        if key not in events:
            events.append(key)
        return self.sem(name)

    def count(self, name, key, batch):
        order = self.order.get(name) or [key]
        return batch * len(order) + (order.index(key) + 1 if key in order else 1)


def advance(streams, phases):
    at = {name: next(stream, None) for name, stream in streams.items()}
    for name, phase in phases:
        if name in at and at[name] == phase:
            at[name] = next(streams[name], None)
    assert not any(at.values()), at


def merge(front, back, follow):
    out = [("back", p) for p in follow.get("start", ())]
    for phase in front:
        out += [("front", phase)] + [("back", p) for p in follow.get(phase, ())]
    assert [p for stream, p in out if stream == "back"] == back
    assert out[-1][0] == "front"
    return out


def gat_mix_program(nc, x, adj, adj_t, w0, a0, wq_t, bq, wk_t, bk, wv_t, bv, wo_t, bo, w2_t, b2, wh, ah, wout,
                    aout, f1, fb1, f2, fb2, gamma, beta, out, order):
    B, N, F = x.shape
    T = N // P
    KF = F // P
    H0 = w0.shape[1]
    H1, D1 = 8, F // 8
    G1 = H1 * D1 // P
    HG = P // D1
    H3 = wh.shape[0]
    SCALE1 = float(D1) ** -0.5
    assert N == 512 and F == 256 and H0 == 128 and G1 == 2

    with ExitStack() as ctx:
        def sb(name, shape, dt=F32):
            return ctx.enter_context(nc.sbuf_tensor(name, shape, dt))

        def new_semaphore(name):
            return ctx.enter_context(nc.semaphore(name))

        sig = Signals(new_semaphore, order)

        def raise_of(batch, name, key=0):
            return sig.sem(name), sig.count(name, key, batch)

        ident = sb("ident", [P, P])
        neg_half = sb("neg_half", [P, T])
        edge_bias = sb("edge_bias", [P, T, N], mybir.dt.bfloat16)
        adj_t_r = sb("adj_t_r", [P, T, N], F32R)
        degree = sb("degree", [P, T])
        has_edge = sb("has_edge", [P, T])
        w0_sb = sb("w0_sb", [P, KF, H0])
        a0_bc = sb("a0_bc", [P, 2, H0])
        wo_sb = sb("wo_sb", [P, KF, F])
        wo3_sb = sb("wo3_sb", [P, H3 * KF, F])
        f1_sb = sb("f1_sb", [P, KF, F])
        f2_sb = sb("f2_sb", [P, KF, F])
        bq_c = sb("bq_c", [P, G1])
        bk_c = sb("bk_c", [P, G1])
        fb1_c = sb("fb1_c", [P, KF])
        rows = {n: sb(n + "_bc", [P, F]) for n in ("bv", "bo", "b2", "fb2", "gamma", "beta")}
        ah_bc = sb("ah_bc", [P, H3, 2, F])
        ao_bc = sb("ao_bc", [P, 2, F])
        split = {}
        for n, src, k, m in (("wq", wq_t, KF, F), ("wk", wk_t, KF, F), ("wv", wv_t, KF, F), ("w2", w2_t, KF, 2 * F),
                             ("wh", wh, KF, H3 * F)):
            split[n] = (src, sb(n + "_hi", [P, k, m], F32R), sb(n + "_lo", [P, k, m], F32R))

        sel = {n: (sb("sel_" + n, [P, HG, len(blocks) * D1], F32R), blocks, low_from)
               for n, blocks, low_from in (("q", (1, 1, 0, 0, 1, 1), 2), ("k", (1, 0, 1, 0, 1), 1))}

        xa = sb("xa", [P, T, F])
        xt = sb("xt", [P, KF, N])
        o_t = xt
        xt_hi, xt_lo = sb("xt_hi", [P, KF, N], F32R), sb("xt_lo", [P, KF, N], F32R)
        vals_a = sb("vals_a", [P, T, F])
        q_st = sb("q_st", [P, HG, N], F32R)
        k_st = sb("k_st", [P, HG, N], F32R)
        qk = {n: k_st[:, i, :] for i, n in enumerate(("q_hi", "q_lo", "k_hi", "k_lo"))}
        m_hi, m_lo = (m[:, 0:2, :].rearrange("p a n -> p (a n)").rearrange("p (t f) -> p t f", f=F) for m in (q_st, k_st))
        xb = sb("xb", [P, T, F])
        xu_hi, xu_lo = sb("xu_hi", [P, KF, N], F32R), sb("xu_lo", [P, KF, N], F32R)
        vals_b = sb("vals_b", [P, 2, T, F])
        h_sb = sb("h_sb", [P, T, F])
        ht = sb("ht", [P, KF, N])

        def two(m, j):
            return m[:, 2 * j:2 * j + 2, :]

        def flat2(m, j):
            return two(m, j).rearrange("p t f -> p (t f)")

        g_row = {s: sb("g_row_" + s, [P, T, N]) for s in "ab"}
        masked = g_row["a"]
        probs = {s: sb("probs_" + s, [P, T, N]) for s in "ab"}
        TURNS = HG + 2
        probs_t = {s: sb("probs_t_" + s, [P, n, N]) for s, n in (("a", TURNS), ("b", T))}
        sums3 = g_row["a"][:, 0:KF, :].rearrange("p a n -> p (a n)").rearrange("p (t f) -> p t f", f=F)
        fs_t = g_row["b"][:].rearrange("p t n -> p (t n)")[:, 0:KF * N].rearrange("p (k n) -> p k n", n=N)
        stage = probs_t["a"][:].rearrange("p a n -> p (a n)")
        sums = sb("sums", [P, T, H1])
        rden = sb("rden", [P, T, H1])
        neg_max = sb("neg_max", [P, T * H1])
        names = ("f_c", "g_c", "g_max", "z_max", "lz_max", "exp_bias", "relu_bias", "sums_g", "rden_g", "var_eps", "rstd")
        row = {s: {n: sb(n + "_" + s, [P, T]) for n in names} for s in "ab"}
        stats = {s: sb("stats_" + s, [P, T, 6]) for s in "ab"}
        mv = {s: sb("mv_" + s, [P, T, 2]) for s in "ab"}

        banks = [ctx.enter_context(nc.psum_tensor(f"bank{i}", [P, 512], F32)) for i in range(8)]
        UNITS = T * HG
        LEAD = 2

        front_list = [("x", 0, k) for k in range(KF)] + ["h0", ("g", 0)] + [("p", 0, t) for t in range(T)] + ["a0"]
        front_list += [("x", 1, k) for k in range(KF)] + ["q0", "k0", "v0", "v1"]
        for g in range(G1):
            if g:
                front_list += [f"q{g}", f"k{g}"]
            front_list += [("stack", g, n, hh) for n in "qk" for hh in range(HG)]
            for n in range(UNITS + LEAD):
                if n < UNITS:
                    front_list.append(("s", g, n))
                if n >= LEAD:
                    front_list.append(("p1", g, n - LEAD))
                    if n - LEAD > HG and (n - LEAD) % HG == 1:
                        front_list.append(("o", g, (n - LEAD) // HG - 1))
            front_list += [("o", g, T - 1), f"r{g}"]
        front_list += ["w0", "w1"] + [("x", 2, k) for k in range(KF)] + ["mj0", "mj1", "mi0", "mi1", ("am", 0), ("am", 1)]
        back_list = [("x", 3, k) for k in range(KF)] + [("wh0", 0), ("wh1", 0), ("g", 1)]
        for h in range(H3 + 1):
            back_list += [("p", 1 + h, t) for t in range(T)]
            if h + 1 < H3:
                back_list += [("wh0", h + 1), ("wh1", h + 1), ("g", 2 + h)]
            back_list += [("a3", h, j) for j in range(2)] + [("x", 4 + h, k) for k in range(KF)]
            if h == H3 - 1:
                back_list.append(("g", 1 + H3))
        back_list += ["f0", "f1", "e0", "e1"]
        FB = 4
        place = {k: i % FB for i, k in enumerate(front_list)} | {k: FB + i % (6 - FB) for i, k in enumerate(back_list)} \
            | {("acc", 0): 6, ("acc", 1): 7}
        nth = {}
        for keys in (front_list, back_list, [("acc", 0), ("acc", 1)]):
            assert len(set(keys)) == len(keys)
            for k in keys:
                nth[k] = [j for j in keys if place[j] == place[k]].index(k)
        per_bank = [sum(p == i for p in place.values()) for i in range(8)]
        full = [new_semaphore(f"bank{i}_full") for i in range(8)]
        drained = [new_semaphore(f"bank{i}_drained") for i in range(8)]

        def bank(key):
            return banks[place[key]]

        def filled(key):
            return full[place[key]]

        def emptied(key):
            return drained[place[key]]

        def stream_of(key):
            return "b" if key in back_list else "a"

        def free(b, key, read=()):
            counts = {}
            for k, n in [(key, nth[key] + 1)] + [(k, nth[k] + 2) for k in read]:
                counts[place[k]] = max(n, counts.get(place[k], 0))
            return [(drained[i], b * per_bank[i] + n) for i, n in counts.items()]

        def product_of(b, key):
            return full[place[key]], b * per_bank[place[key]] + (nth[key] + 1)

        def moved(b, key):
            return drained[place[key]], b * per_bank[place[key]] + (nth[key] + 2)

        front = ["x0", "h0", ("g0", 0), ("g0", 1), ("score0", 0), ("score0", 1), "p0", "a0", "stats0", "norm0", "x1", "q0", "v"]
        for g in range(G1):
            front += ([f"q{g}"] if g else []) + [("stack", g)] + [("unit", g, n) for n in range(UNITS + LEAD)] \
                + [("o", g), ("r", g)]
        front += [("w", 0), ("w", 1), "stats1", "norm1", "x2", "mj", "mi", "am", "stats2", "norm2"]
        back = ["x3", ("wh", 0)] + [(n, 0, half) for n in ("g3", "score3") for half in range(2)]
        for h in range(H3 + 1):
            back += [("p3", h)] + ([("wh", h + 1), ("g3", h + 1, 0), ("g3", h + 1, 1)] if h + 1 < H3 else [])
            back += [("a3", h, 0), ("a3", h, 1)]
            back += ([("score3", h + 1, 0), ("score3", h + 1, 1)] if h + 1 < H3 else []) + [("ht", h)]
            back += [("acc", h, 0), ("acc", h, 1)] if h < H3 else []
            if h == H3 - 1:
                back += [("values", H3)] + [(n, H3, half) for n in ("g3", "score3") for half in range(2)]
        back += [("f", 0), ("f", 1), ("e", 0), ("e", 1), "stats3", "norm3", "stats4", "norm4"]
        follow = {"h0": ["x3"], ("g0", 1): [("wh", 0)], ("score0", 0): [("g3", 0, 0)],
                  "p0": [("g3", 0, 1), ("score3", 0, 0), ("score3", 0, 1)], "norm0": [("p3", 0)], "x1": [("wh", 1)],
                  "v": [("g3", 1, 0), ("g3", 1, 1), ("a3", 0, 0), ("a3", 0, 1)], ("stack", 0): [("score3", 1, 0)],
                  ("unit", 0, 6): [("score3", 1, 1), ("ht", 0)], ("unit", 0, 8): [("acc", 0, 0)],
                  ("unit", 0, 12): [("acc", 0, 1), ("p3", 1)], ("unit", 0, 14): [("wh", 2)],
                  ("unit", 0, 16): [("g3", 2, 0), ("g3", 2, 1), ("a3", 1, 0), ("a3", 1, 1)],
                  ("o", 0): [("score3", 2, 0), ("score3", 2, 1), ("ht", 1)],
                  "q1": [("acc", 1, 0), ("acc", 1, 1), ("p3", 2), ("wh", 3)], ("stack", 1): [("g3", 3, 0)],
                  ("unit", 1, 1): [("g3", 3, 1), ("a3", 2, 0), ("a3", 2, 1)], ("unit", 1, 4): [("score3", 3, 0)],
                  ("unit", 1, 5): [("score3", 3, 1), ("ht", 2)], ("unit", 1, 7): [("acc", 2, 0)],
                  ("unit", 1, 8): [("acc", 2, 1), ("p3", 3)], ("unit", 1, 9): [("a3", 3, 0)],
                  ("unit", 1, 10): [("a3", 3, 1)], ("unit", 1, 12): [("ht", 3)],
                  ("unit", 1, 15): [("acc", 3, 0), ("acc", 3, 1), ("values", 4)], ("o", 1): [("g3", 4, 0)],
                  ("r", 1): [("g3", 4, 1), ("score3", 4, 0), ("score3", 4, 1)], "stats1": [("p3", 4)],
                  "norm1": [("a3", 4, 0)], "x2": [("a3", 4, 1)], "mj": [("ht", 4), ("f", 0), ("f", 1)],
                  "mi": [("e", 0), ("e", 1), "stats3", "norm3", "stats4", "norm4"]}
        merged = merge(front, back, follow)

        def both(front_stream, back_stream, fori):
            advance({"front": front_stream(0)}, [("front", p) for p in front])
            with fori(0, B - 1) as b:
                advance({"front": front_stream(b + 1), "back": back_stream(b)}, merged)
            advance({"back": back_stream(B - 1)}, [("back", p) for p in back])

        def leaky_of(idx):
            if idx == 0:
                return "a", SLOPE_0, vals_a[:, :, 0:H0], lambda j: a0_bc[:, j, :]
            return "b", SLOPE_3, vals_b[:, (idx - 1) % 2], \
                (lambda j: ah_bc[:, idx - 1, j, :]) if idx <= H3 else (lambda j: ao_bc[:, j, :])

        def bank2(key):
            return bank(key)[:].rearrange("p (t f) -> p t f", f=F)

        def row2(n):
            return rows[n][:].unsqueeze(1).to_broadcast([P, 2, F])

        loaded = new_semaphore("loaded")
        x_loaded = new_semaphore("x_loaded")
        stored = new_semaphore("stored")
        staged = new_semaphore("staged")
        constants = new_semaphore("constants")
        waits_taken = new_semaphore("waits_taken")
        sp_waits_taken = new_semaphore("sp_waits_taken")
        split_hi = new_semaphore("split_hi")
        ready = new_semaphore("setup_ready")
        READY = 3

        pieces = []
        for n, (src, hi, _) in split.items():
            k, m = hi.shape[1], hi.shape[2]
            step = max(1, T * N // m)
            pieces += [(n, a, min(a + step, k)) for a in range(0, k, step)]
        NP_ = len(pieces)
        N_CONST = 4 + sum(len(blocks) for _, blocks, _ in sel.values())
        small_loads = []

        block = ctx.enter_context(nc.Block())

        @block.sync
        def _(sp):
            sp.sem_inc(stored, 16)

            def load(dst, src, **kw):
                sp.dma_start(dst, src, **kw).then_inc(loaded, 16)
                small_loads.append(1)

            sp.dma_start(xa[:], x[0].rearrange("(t p) f -> p t f", p=P)).then_inc(x_loaded, 16)
            load(g_row["b"][:].bitcast(mybir.dt.int32), adj.rearrange("(t p) n -> p t n", p=P))
            load(probs["b"][:].bitcast(mybir.dt.int32), adj_t.rearrange("(t p) n -> p t n", p=P))
            load(w0_sb[:], w0.rearrange("(k p) n -> p k n", p=P))
            load(wo_sb[:], wo_t.rearrange("(k p) n -> p k n", p=P))
            load(wo3_sb[:], wout.rearrange("(k p) n -> p k n", p=P))
            load(f1_sb[:], f1.rearrange("(k p) n -> p k n", p=P))
            load(f2_sb[:], f2.rearrange("(k p) n -> p k n", p=P))
            load(bq_c[:], bq.rearrange("(k p) -> p k", p=P), allow_slow_non_contiguous=True)
            load(bk_c[:], bk.rearrange("(k p) -> p k", p=P), allow_slow_non_contiguous=True)
            load(fb1_c[:], fb1.rearrange("(k p) -> p k", p=P), allow_slow_non_contiguous=True)
            for n, src in (("bv", bv), ("bo", bo), ("b2", b2), ("fb2", fb2), ("gamma", gamma), ("beta", beta)):
                load(rows[n][:], src.partition_broadcast(P))
            for j in range(2):
                load(a0_bc[:, j, :], a0[j].rearrange("n o -> (n o)").partition_broadcast(P))
                load(ao_bc[:, j, :], aout[j * F:(j + 1) * F].partition_broadcast(P))
            for h in range(H3):
                load(ah_bc[:, h].rearrange("p j f -> p (j f)"), ah[h].partition_broadcast(P))
            for i, (n, a, z) in enumerate(pieces):
                if i:
                    sp.wait_ge(constants, i)
                src, hi, _ = split[n]
                m = hi.shape[2]
                dst = stage[:, 0:(z - a) * m].rearrange("p (k n) -> p k n", n=m)
                if n == "wh":
                    for k in range(a, z):
                        sp.dma_start(dst[:, k - a, :].rearrange("p (h o) -> p h o", h=H3),
                                     src[:, k * P:(k + 1) * P, :].rearrange("h p o -> p h o")).then_inc(staged, 16)
                else:
                    sp.dma_start(dst, src.rearrange("(k p) n -> p k n", p=P)[:, a:z, :]).then_inc(staged, 16)

            def store(b):
                sp.wait_ge(*raise_of(b, "norm_b", (4, T - 1)))
                sp.sem_inc(sp_waits_taken, 1)
                sp.dma_start(out[b].rearrange("(t p) f -> p t f", p=P), h_sb[:]).then_inc(stored, 16)

            def next_x(b):
                sp.wait_ge(*moved(b, "mi1"))
                sp.sem_inc(sp_waits_taken, 1)
                sp.dma_start(xa[:], x[b + 1].rearrange("(t p) f -> p t f", p=P)).then_inc(x_loaded, 16)

            next_x(0)
            with sp.Fori(0, B - 2) as b:
                store(b)
                next_x(b + 1)
            store(B - 2)
            store(B - 1)
            sp.wait_ge(stored, 16 * B + 16)

        N_LOADS = len(small_loads)
        n_staged = []
        for n, a, z in pieces:
            n_staged.append((n_staged[-1] if n_staged else 0) + 16 * ((z - a) if n == "wh" else 1))

        @block.gpsimd
        def _(pool):
            pool.memset(ident[:], 0.0).then_inc(ready, 1)
            pool.wait_ge(ready, 1)
            pool.affine_select(out=ident[:], in_=ident[:], compare_op=ALU.not_equal, fill=1.0, base=0,
                               pattern=[[-1, P]], channel_multiplier=1).then_inc(ready, 1)
            pool.memset(neg_half[:], -0.5).then_inc(ready, 1)
            pool.wait_ge(ready, READY)
            pool.wait_ge(constants, NP_ + N_CONST)
            pool.wait_ge(loaded, 16 * N_LOADS)

            def root(b, n):
                s = "a" if n < 3 else "b"
                pool.wait_ge(*raise_of(b, "var_" + s, n))
                pool.tensor_tensor(row[s]["rstd"][:], row[s]["var_eps"][:], neg_half[:], ALU.pow)\
                    .then_inc(sig.raised("rstd_" + s, n), 1)

            def add_row(b, n, dst, transposed):
                for k in range(KF):
                    pool.wait_ge(*product_of(b, ("x", transposed, k)))
                for j in range(2):
                    pool.tensor_tensor(two(dst, j), two(dst, j), row2(n), ALU.add).then_inc(sig.raised("with_" + n, j), 1)

            def front_stream(b):
                yield "stats0"
                root(b, 0)
                yield "stack", 0
                add_row(b, "bo", xa, 1)
                yield "stats1"
                root(b, 1)
                yield "mj"
                for k in range(KF):
                    pool.wait_ge(*product_of(b, ("x", 2, k)))
                scaled = probs["a"][:, :, 0:F]
                for j in range(2):
                    pool.tensor_tensor(two(scaled, j), row2("b2"),
                                       degree[:, 2 * j:2 * j + 2].unsqueeze(2).to_broadcast([P, 2, F]), ALU.mult)\
                        .then_inc(sig.raised("degree_b2", j), 1)
                for j in range(2):
                    pool.wait_ge(*raise_of(b, "degree_b2", j))
                    pool.tensor_tensor(two(xa, j), two(xa, j), two(scaled, j), ALU.add).then_inc(sig.raised("with_b2", j), 1)
                yield "stats2"
                root(b, 2)

            def back_stream(b):
                yield "g3", 0, 0
                add_row(b, "beta", xb, 3)
                yield "f", 0
                add_row(b, "fb2", h_sb, 4 + H3)
                yield "stats3"
                root(b, 3)
                yield "stats4"
                root(b, 4)

            both(front_stream, back_stream, pool.Fori)

        @block.tensor
        def _(pe):
            pe.wait_ge(ready, READY)
            pe.wait_ge(constants, NP_ + N_CONST)
            pe.wait_ge(loaded, 16 * N_LOADS)
            for bank_drained in drained:
                pe.sem_inc(bank_drained, 1)

            def transpose_x(b, n, src, wait_tile):
                for k in range(KF):
                    for count in free(b, ("x", n, k)):
                        pe.wait_ge(*count)
                    for t in range(T):
                        if k == 0 and wait_tile:
                            wait_tile(t)
                        last = pe.transpose(bank(("x", n, k))[:, t * P:(t + 1) * P], src[:, t, k * P:(k + 1) * P], ident[:])
                    last.then_inc(filled(("x", n, k)), 1)

            def product3(dst, lhs, rhs, ks):
                for k in range(ks):
                    for i, (a, z) in enumerate([(0, 0), (0, 1), (1, 0)]):
                        last = pe.matmul(dst, lhs[a](k), rhs[z](k), start=k == 0 and i == 0,
                                         stop=k == ks - 1 and i == 2)
                return last

            def token_product(b, keys, xs, w, lo, read=()):
                for j, key in enumerate(keys):
                    for count in free(b, key, () if j else read):
                        pe.wait_ge(*count)
                    for t in (2 * j, 2 * j + 1):
                        last = product3(bank(key)[:, (t % 2) * F:(t % 2 + 1) * F],
                                        [lambda k, m=m: m[:, k, t * P:(t + 1) * P] for m in xs],
                                        [lambda k, m=m: m[:, k, lo:lo + F] for m in split[w][1:]], KF)
                    last.then_inc(filled(key), 1)

            def broadcast_g(b, idx):
                s, key = leaky_of(idx)[0], ("g", idx)
                for count in free(b, key):
                    pe.wait_ge(*count)
                pe.wait_ge(*raise_of(b, "dots_" + s, (idx, T - 1, 1)))
                for t in range(T):
                    last = pe.matmul(bank(key)[:, t * P:(t + 1) * P], row[s]["g_c"][:, t:t + 1].to_broadcast([P, P]), ident[:],
                                     start=True, stop=True)
                last.then_inc(filled(key), 1)

            def transpose_probs(b, key, src, name, event):
                for count in free(b, key):
                    pe.wait_ge(*count)
                pe.wait_ge(*raise_of(b, name, event))
                for j in range(T):
                    last = pe.transpose(bank(key)[:, j * P:(j + 1) * P], src[:, j * P:(j + 1) * P], ident[:])
                last.then_inc(filled(key), 1)

            def qk_product(b, g):
                for n in "qk":
                    key = f"{n}{g}"
                    for count in free(b, key, [("x", 1, k) for k in range(KF)] if key == "q0" else ()):
                        pe.wait_ge(*count)
                    last = product3(bank(key)[:], [lambda k, m=m: m[:, k, g * P:(g + 1) * P] for m in split["w" + n][1:]],
                                    [lambda k, m=m: m[:, k, :] for m in (xt_hi, xt_lo)], KF)
                    last.then_inc(filled(key), 1)

            def stack(b, g):
                for n in "qk":
                    for hh in range(HG):
                        key, (ones, _, low_from) = ("stack", g, n, hh), sel[n]
                        for count in free(b, key, [f"{n}{g}"]):
                            pe.wait_ge(*count)
                        pe.matmul(bank(key)[:], ones[:, hh, 0:P], qk[n + "_hi"], start=True, stop=False)
                        pe.matmul(bank(key)[:], ones[:, hh, low_from * D1:low_from * D1 + P], qk[n + "_lo"], start=False,
                                  stop=True).then_inc(filled(key), 1)

            def scores(b, g, n):
                t, hh, key = n // HG, n % HG, ("s", g, n)
                for count in free(b, key, [("stack", g, m, i) for m in "qk" for i in range(HG)] if n == 0 else ()):
                    pe.wait_ge(*count)
                pe.matmul(bank(key)[:], q_st[:, hh, t * P:(t + 1) * P], k_st[:, hh, :], start=True, stop=True)\
                  .then_inc(filled(key), 1)

            def weigh(b, g, t):
                key = ("o", g, t)
                for count in free(b, key, ["v0", "v1"] + [("p1", g, t * HG + hh) for hh in range(HG)]):
                    pe.wait_ge(*count)
                for j in range(T):
                    for hh in range(HG):
                        h = g * HG + hh
                        last = pe.matmul(bank(key)[hh * D1:(hh + 1) * D1, 0:P], vals_a[:, j, h * D1:(h + 1) * D1],
                                         probs_t["a"][:, (t * HG + hh) % TURNS, j * P:(j + 1) * P], start=j == 0, stop=j == T - 1)
                last.then_inc(filled(key), 1)

            def front_stream(b):
                yield "x0"
                pe.wait_ge(x_loaded, b * 16 + 16)
                transpose_x(b, 0, xa, None)
                yield "h0"
                for count in free(b, "h0", [("x", 0, k) for k in range(KF)]):
                    pe.wait_ge(*count)
                for t in range(T):
                    for k in range(KF):
                        last = pe.matmul(bank("h0")[:, t * P:(t + 1) * P], xt[:, k, t * P:(t + 1) * P], w0_sb[:, k, :],
                                         start=k == 0, stop=k == KF - 1)
                last.then_inc(filled("h0"), 1)
                yield "g0", 0
                broadcast_g(b, 0)
                yield "p0"
                for t in range(T):
                    transpose_probs(b, ("p", 0, t), probs["a"][:, t, :], "probs_g_a", (0, t))
                yield "a0"
                for count in free(b, "a0", [("p", 0, t) for t in range(T)]):
                    pe.wait_ge(*count)
                for t in range(T):
                    for j in range(T):
                        last = pe.matmul(bank("a0")[:, t * P:(t + 1) * P], probs_t["a"][:, t, j * P:(j + 1) * P],
                                         vals_a[:, j, 0:H0], start=j == 0, stop=j == T - 1)
                last.then_inc(filled("a0"), 1)

                yield "x1"
                transpose_x(b, 1, xa, lambda t: pe.wait_ge(*raise_of(b, "norm_a", (0, t))))
                yield "q0"
                qk_product(b, 0)
                yield "v"
                token_product(b, ["v0", "v1"], (xt_hi, xt_lo), "wv", 0)
                for g in range(G1):
                    if g:
                        yield f"q{g}"
                        qk_product(b, g)
                    yield "stack", g
                    stack(b, g)
                    for n in range(UNITS + LEAD):
                        yield "unit", g, n
                        if n < UNITS:
                            scores(b, g, n)
                        m = n - LEAD
                        if m >= 0:
                            transpose_probs(b, ("p1", g, m), probs["a"][:, m % T, :], "probs1", (g, m))
                        if m > HG and m % HG == 1:
                            weigh(b, g, m // HG - 1)
                    yield "o", g
                    weigh(b, g, T - 1)
                    yield "r", g
                    key = f"r{g}"
                    for count in free(b, key):
                        pe.wait_ge(*count)
                    pe.wait_ge(*raise_of(b, "rden1", g))
                    for t in range(T):
                        for hh in range(HG):
                            last = pe.matmul(bank(key)[hh * D1:(hh + 1) * D1, t * P:(t + 1) * P],
                                             rden[:, t, g * HG + hh:g * HG + hh + 1].to_broadcast([P, D1]), ident[:],
                                             start=True, stop=True)
                    last.then_inc(filled(key), 1)
                for j in range(2):
                    yield "w", j
                    key = f"w{j}"
                    for count in free(b, key, [f"r{g}" for g in range(G1)]):
                        pe.wait_ge(*count)
                    for t in (2 * j, 2 * j + 1):
                        for k in range(KF):
                            last = pe.matmul(bank(key)[:, (t % 2) * F:(t % 2 + 1) * F], o_t[:, k, t * P:(t + 1) * P],
                                             wo_sb[:, k, :], start=k == 0, stop=k == KF - 1)
                    last.then_inc(filled(key), 1)

                yield "x2"
                transpose_x(b, 2, xa, lambda t: pe.wait_ge(*raise_of(b, "norm_a", (1, t))))
                yield "mj"
                token_product(b, ["mj0", "mj1"], (xt_hi, xt_lo), "w2", F, [("x", 2, k) for k in range(KF)])
                yield "mi"
                token_product(b, ["mi0", "mi1"], (xt_hi, xt_lo), "w2", 0)
                yield "am"
                for j in range(2):
                    key = ("am", j)
                    for count in free(b, key, ["mj0", "mj1"]):
                        pe.wait_ge(*count)
                    for t in (2 * j, 2 * j + 1):
                        for c in range(T):
                            for m in (m_hi, m_lo):
                                last = pe.matmul(bank(key)[:, (t % 2) * F:(t % 2 + 1) * F], adj_t_r[:, c, t * P:(t + 1) * P],
                                                 m[:, c, :], start=c == 0 and m is m_hi, stop=c == T - 1 and m is m_lo)
                    last.then_inc(filled(key), 1)

            def back_stream(b):
                def head_values(h):
                    token_product(b, [("wh0", h), ("wh1", h)], (xu_hi, xu_lo), "wh", h * F,
                                  () if h else [("x", 3, k) for k in range(KF)])

                yield "x3"
                transpose_x(b, 3, xb, lambda t: pe.wait_ge(*raise_of(b, "norm_a", (2, t))))
                yield "wh", 0
                head_values(0)
                yield "g3", 0, 0
                broadcast_g(b, 1)
                for h in range(H3 + 1):
                    yield "p3", h
                    for t in range(T):
                        transpose_probs(b, ("p", 1 + h, t), probs["b"][:, t, :], "probs_g_b", (1 + h, t))
                    if h + 1 < H3:
                        yield "wh", h + 1
                        head_values(h + 1)
                        yield "g3", h + 1, 0
                        broadcast_g(b, 2 + h)
                    for j in range(2):
                        yield "a3", h, j
                        key = ("a3", h, j)
                        for count in free(b, key, [("p", 1 + h, t) for t in (2 * j, 2 * j + 1)]):
                            pe.wait_ge(*count)
                        for t in (2 * j, 2 * j + 1):
                            for c in range(T):
                                last = pe.matmul(bank(key)[:, (t % 2) * F:(t % 2 + 1) * F],
                                                 probs_t["b"][:, t, c * P:(c + 1) * P], vals_b[:, h % 2, c, :],
                                                 start=c == 0, stop=c == T - 1)
                        last.then_inc(filled(key), 1)
                    yield "ht", h
                    transpose_x(b, 4 + h, h_sb, lambda t: pe.wait_ge(*moved(b, ("a3", h, t // 2))))
                    if h < H3:
                        for j in range(2):
                            yield "acc", h, j
                            if h == 0:
                                for count in free(b, ("acc", j), [("x", 4, k) for k in range(KF)]):
                                    pe.wait_ge(*count)
                            elif j == 0:
                                for k in range(KF):
                                    pe.wait_ge(*moved(b, ("x", 4 + h, k)))
                            for t in (2 * j, 2 * j + 1):
                                for k in range(KF):
                                    last = pe.matmul(bank(("acc", j))[:, (t % 2) * F:(t % 2 + 1) * F],
                                                     ht[:, k, t * P:(t + 1) * P], wo3_sb[:, h * KF + k, :],
                                                     start=h == 0 and t % 2 == 0 and k == 0,
                                                     stop=h == H3 - 1 and t % 2 == 1 and k == KF - 1,
                                                     skip_group_check=True)
                            if h == H3 - 1:
                                last.then_inc(filled(("acc", j)), 1)
                            elif j == 1:
                                last.then_inc(sig.raised("gathered", h), 1)
                    if h == H3 - 1:
                        yield "g3", H3, 0
                        broadcast_g(b, 1 + H3)
                for m_ in range(KF):
                    yield "f", m_
                    key = f"f{m_}"
                    for count in free(b, key, [("x", 4 + H3, k) for k in range(KF)]):
                        pe.wait_ge(*count)
                    for k in range(KF):
                        last = pe.matmul(bank(key)[:], f1_sb[:, k, m_ * P:(m_ + 1) * P], ht[:, k, :], start=k == 0,
                                         stop=k == KF - 1)
                    last.then_inc(filled(key), 1)
                for j in range(2):
                    yield "e", j
                    key = f"e{j}"
                    for count in free(b, key, [f"f{m_}" for m_ in range(KF)]):
                        pe.wait_ge(*count)
                    for t in (2 * j, 2 * j + 1):
                        for k in range(KF):
                            last = pe.matmul(bank(key)[:, (t % 2) * F:(t % 2 + 1) * F], fs_t[:, k, t * P:(t + 1) * P],
                                             f2_sb[:, k, :], start=k == 0, stop=k == KF - 1)
                    last.then_inc(filled(key), 1)

            both(front_stream, back_stream, pe.Fori)

        @block.scalar
        def _(act):
            act.wait_ge(constants, NP_ + N_CONST)
            act.wait_ge(loaded, 16 * N_LOADS)

            def drain(b, key, dst, func=ACT.Copy, src=None, **kw):
                act.wait_ge(*product_of(b, key))
                act.activation(dst, bank(key)[:] if src is None else src, func, **kw).then_inc(emptied(key), 1)

            def high(b, key, dst, func=ACT.Copy, **kw):
                act.wait_ge(*product_of(b, key))
                act.activation(dst, bank(key)[:], func, **kw).then_inc(sig.raised("high_" + stream_of(key), key), 1)

            def relus(b, idx, half):
                s, slope, _, _ = leaky_of(idx)
                for t in (2 * half, 2 * half + 1):
                    if t < T - 1:
                        act.wait_ge(*raise_of(b, "masked_g_" + s, (idx, t)))
                    else:
                        act.wait_ge(*moved(b, ("g", idx)))
                    if t == 0:
                        act.wait_ge(*raise_of(b, "relu_bias_" + s, idx))
                    if idx > 1:
                        act.wait_ge(*product_of(b, ("p", idx - 1, t)))
                    act.activation(probs[s][:, t, :], g_row[s][:, t, :], ACT.Relu, bias=row[s]["relu_bias"][:, t:t + 1],
                                   scale=1 - slope).then_inc(sig.raised("relu_" + s, (idx, t)), 1)

            def exps(b, idx, half):
                s = leaky_of(idx)[0]
                for t in (2 * half, 2 * half + 1):
                    act.wait_ge(*raise_of(b, "score_" + s, (idx, t)))
                    act.activation(probs[s][:, t, :], g_row[s][:, t, :], ACT.Exp, bias=row[s]["exp_bias"][:, t:t + 1],
                                   accum_out=row[s]["sums_g"][:, t:t + 1]).then_inc(sig.raised("probs_g_" + s, (idx, t)), 1)

            def exp1(b, g, n):
                t, h = n // HG, g * HG + n % HG
                act.wait_ge(*moved(b, ("s", g, n)))
                if n >= T:
                    act.wait_ge(*product_of(b, ("p1", g, n - T)))
                elif g:
                    act.wait_ge(*product_of(b, ("p1", g - 1, n + UNITS - T)))
                act.activation(probs["a"][:, n % T, :], masked[:, n % T, :], ACT.Exp,
                               bias=neg_max[:, g * UNITS + n:g * UNITS + n + 1], scale=-1.0,
                               accum_out=sums[:, t, h:h + 1]).then_inc(sig.raised("probs1", (g, n)), 1)

            def front_stream(b):
                yield "x0"
                for k in range(KF):
                    drain(b, ("x", 0, k), xt[:, k, :])
                yield "h0"
                drain(b, "h0", vals_a[:, :, 0:H0], src=bank("h0")[:].rearrange("p (t n) -> p t n", n=H0))
                for half in range(2):
                    yield "g0", half
                    relus(b, 0, half)
                for half in range(2):
                    yield "score0", half
                    exps(b, 0, half)
                yield "p0"
                for t in range(T):
                    drain(b, ("p", 0, t), probs_t["a"][:, t, :])
                yield "x1"
                for k in range(KF):
                    high(b, ("x", 1, k), xt_hi[:, k, :])
                yield "q0"
                high(b, "q0", qk["q_hi"], ACT.Identity, bias=bq_c[:, 0:1])
                high(b, "k0", qk["k_hi"], ACT.Identity, bias=bk_c[:, 0:1])
                for g in range(G1):
                    if g:
                        yield f"q{g}"
                        act.wait_ge(*product_of(b, ("s", g - 1, UNITS - 1)))
                        high(b, f"q{g}", qk["q_hi"], ACT.Identity, bias=bq_c[:, g:g + 1])
                        high(b, f"k{g}", qk["k_hi"], ACT.Identity, bias=bk_c[:, g:g + 1])
                    yield "stack", g
                    for hh in range(HG):
                        drain(b, ("stack", g, "q", hh), q_st[:, hh, :])
                    for n in range(UNITS + LEAD):
                        yield "unit", g, n
                        if n < UNITS:
                            exp1(b, g, n)
                        m = n - LEAD
                        if m >= 0:
                            if m >= TURNS and m % HG == TURNS % HG:
                                t = (m - TURNS) // HG
                                drain(b, ("o", g, t), o_t[:, g, t * P:(t + 1) * P], src=bank(("o", g, t))[:, 0:P])
                            elif m == 0 and g:
                                act.wait_ge(*product_of(b, ("o", g - 1, T - 1)))
                            drain(b, ("p1", g, m), probs_t["a"][:, m % TURNS, :])
                    yield "o", g
                    drain(b, ("o", g, T - 1), o_t[:, g, (T - 1) * P:], src=bank(("o", g, T - 1))[:, 0:P])
                yield "x2"
                for k in range(KF):
                    high(b, ("x", 2, k), xt_hi[:, k, :])
                yield "mj"
                for j in range(2):
                    high(b, f"mj{j}", flat2(m_hi, j))

            def back_stream(b):
                def move_values(h):
                    for j in range(2):
                        key = (f"wh{j}", h) if h < H3 else ("acc", j)
                        if j == 0 and h >= 2:
                            act.wait_ge(*product_of(b, ("a3", h - 2, 1)))
                        drain(b, key, flat2(vals_b[:, h % 2], j))

                yield "x3"
                for k in range(KF):
                    high(b, ("x", 3, k), xu_hi[:, k, :])
                yield "wh", 0
                move_values(0)
                for half in range(2):
                    yield "g3", 0, half
                    relus(b, 1, half)
                for half in range(2):
                    yield "score3", 0, half
                    exps(b, 1, half)
                for h in range(H3 + 1):
                    yield "p3", h
                    for t in range(T):
                        if h and t == 0:
                            act.wait_ge(*product_of(b, ("a3", h - 1, 1)))
                        drain(b, ("p", 1 + h, t), probs_t["b"][:, t, :])
                    if h + 1 < H3:
                        yield "wh", h + 1
                        move_values(h + 1)
                        for half in range(2):
                            yield "g3", h + 1, half
                            relus(b, 2 + h, half)
                    for j in range(2):
                        yield "a3", h, j
                        key = ("a3", h, j)
                        act.wait_ge(*product_of(b, key))
                        act.wait_ge(*raise_of(b, "rden_g_b", 1 + h))
                        if h == 0 and j == 0:
                            act.wait_ge(stored, b * 16 + 16)
                        elif h and j == 0:
                            for k in range(KF):
                                act.wait_ge(*product_of(b, ("x", 3 + h, k)))
                        for i in range(2):
                            t = 2 * j + i
                            act.activation(h_sb[:, t, :], bank2(key)[:, i, :], ACT.Exp, scale=row["b"]["rden_g"][:, t:t + 1])\
                               .then_inc(sig.raised("elu_exp", (h, t)), 1)
                    if h + 1 < H3:
                        for half in range(2):
                            yield "score3", h + 1, half
                            exps(b, 2 + h, half)
                    yield "ht", h
                    for k in range(KF):
                        drain(b, ("x", 4 + h, k), ht[:, k, :])
                    if h == H3 - 1:
                        yield "values", H3
                        move_values(H3)
                        for half in range(2):
                            yield "g3", H3, half
                            relus(b, 1 + H3, half)
                        for half in range(2):
                            yield "score3", H3, half
                            exps(b, 1 + H3, half)
                for m in range(KF):
                    yield "f", m
                    drain(b, f"f{m}", fs_t[:, m, :], ACT.Relu, bias=fb1_c[:, m:m + 1])

            both(front_stream, back_stream, act.Fori)

        @block.vector
        def _(dve):
            dve.wait_ge(loaded, 16 * N_LOADS)
            for i, (n, a, z) in enumerate(pieces):
                _, hi, lo = split[n]
                m = hi.shape[2]
                src = stage[:, 0:(z - a) * m].rearrange("p (k n) -> p k n", n=m)
                dve.wait_ge(staged, n_staged[i])
                dve.tensor_copy(hi[:, a:z, :], src).then_inc(split_hi, 1)
                dve.wait_ge(split_hi, i + 1)
                dve.tensor_tensor(lo[:, a:z, :], src, hi[:, a:z, :].bitcast(F32), ALU.subtract).then_inc(constants, 1)
            adj_i, adj_ti = (m["b"][:].bitcast(mybir.dt.int32) for m in (g_row, probs))
            dve.tensor_copy(adj_t_r[:], adj_ti).then_inc(constants, 1)
            dve.tensor_scalar(edge_bias[:], adj_i, -NO_EDGE, NO_EDGE, ALU.mult, ALU.add).then_inc(constants, 1)
            dve.tensor_reduce(degree[:], adj_i, AX_X, ALU.add).then_inc(constants, 1)
            dve.wait_ge(ready, READY)
            for ones, blocks, _ in sel.values():
                for c, one in enumerate(blocks):
                    dve.tensor_scalar(ones[:, :, c * D1:(c + 1) * D1], ident[:].rearrange("p (h d) -> p h d", d=D1), float(one),
                                      None, ALU.mult).then_inc(constants, 1)
            dve.wait_ge(constants, NP_ + N_CONST - 1)
            dve.tensor_scalar(has_edge[:], degree[:], 1.0, None, ALU.min).then_inc(constants, 1)
            dve.wait_ge(constants, NP_ + N_CONST)

            def settled():
                dve.sem_inc(waits_taken, 1)

            def low(b, key, dst, hi, bias=None):
                dve.wait_ge(*raise_of(b, "high_" + stream_of(key), key))
                if bias is None:
                    dve.tensor_tensor(dst, bank(key)[:], hi.bitcast(F32), ALU.subtract).then_inc(emptied(key), 1)
                else:
                    dve.scalar_tensor_tensor(dst, bank(key)[:], bias, hi.bitcast(F32), ALU.add, ALU.subtract)\
                       .then_inc(emptied(key), 1)

            def norm_stats(b, n, s, src):
                for t in range(T):
                    dve.bn_stats(stats[s][:, t, :], src[:, t, :]).then_inc(sig.raised("stats_" + s, (n, t)), 1)
                for t in range(T):
                    dve.wait_ge(*raise_of(b, "stats_" + s, (n, t)))
                    settled()
                    dve.bn_aggr(mv[s][:, t, :], stats[s][:, t, :]).then_inc(sig.raised("mean_var_" + s, (n, t)), 1)
                dve.wait_ge(*raise_of(b, "mean_var_" + s, (n, T - 1)))
                dve.tensor_scalar(row[s]["var_eps"][:], mv[s][:, :, 1], EPS, None, ALU.add).then_inc(sig.raised("var_" + s, n), 1)

            def norm(b, n, s, src, dst):
                dve.wait_ge(*raise_of(b, "rstd_" + s, n))
                for t in range(T):
                    dve.tensor_scalar(dst[:, t, :], src[:, t, :], mv[s][:, t, 0:1], row[s]["rstd"][:, t:t + 1], ALU.subtract,
                                      ALU.mult).then_inc(sig.raised("norm_" + s, (n, t)), 1)

            def row_dots(b, idx):
                s, _, vals, a_of = leaky_of(idx)
                width = vals.shape[-1]
                for key in ["h0"] if idx == 0 else [(f"wh{j}", idx - 1) for j in range(2)] if idx <= H3 else \
                        [("acc", j) for j in range(2)]:
                    dve.wait_ge(*moved(b, key))
                if idx == 0 and not isinstance(b, int):
                    dve.wait_ge(*raise_of(b - 1, "norm_a", (2, T - 1)))
                for t in range(T):
                    for j in range(2):
                        if idx > 1 and j == 0:
                            dve.wait_ge(*raise_of(b, "probs_g_" + s, (idx - 1, t)))
                        dve.tensor_tensor_reduce(g_row[s][:, t, j * width:(j + 1) * width], vals[:, t, :], a_of(j), 1.0, 0.0,
                                                 ALU.mult, ALU.add, row[s]["fg"[j] + "_c"][:, t:t + 1])\
                           .then_inc(sig.raised("dots_" + s, (idx, t, j)), 1)

            def mask_rows(b, idx, half):
                s, slope, _, _ = leaky_of(idx)
                key, r = ("g", idx), row[s]
                if half == 0:
                    dve.wait_ge(*raise_of(b, "dots_" + s, (idx, T - 1, 1)))
                    dve.tensor_scalar(r["relu_bias"][:], r["f_c"][:], 1 - slope, None, ALU.mult)\
                       .then_inc(sig.raised("relu_bias_" + s, idx), 1)
                for t in (2 * half, 2 * half + 1):
                    if t == 0:
                        dve.wait_ge(*product_of(b, key))
                        settled()
                    sem = emptied(key) if t == T - 1 else sig.raised("masked_g_" + s, (idx, t))
                    dve.tensor_tensor_reduce(g_row[s][:, t, :], bank(key)[:], edge_bias[:, t, :], 1.0, START_MAX,
                                             ALU.add, ALU.max, r["g_max"][:, t:t + 1]).then_inc(sem, 1)
                if half == 0:
                    return
                dve.wait_ge(*moved(b, key))
                dve.tensor_tensor(r["z_max"][:], r["g_max"][:], r["f_c"][:], ALU.add).then_inc(sig.raised("z_max_" + s, idx), 1)
                dve.wait_ge(*raise_of(b, "z_max_" + s, idx))
                dve.scalar_tensor_tensor(r["lz_max"][:], r["z_max"][:], slope, r["z_max"][:], ALU.mult, ALU.max)\
                   .then_inc(sig.raised("lz_max_" + s, idx), 1)
                dve.wait_ge(*raise_of(b, "lz_max_" + s, idx))
                dve.scalar_tensor_tensor(r["exp_bias"][:], r["f_c"][:], slope, r["lz_max"][:], ALU.mult, ALU.subtract)\
                   .then_inc(sig.raised("exp_bias_" + s, idx), 1)

            def score_rows(b, idx, half):
                s, slope, _, _ = leaky_of(idx)
                for t in (2 * half, 2 * half + 1):
                    dve.wait_ge(*raise_of(b, "relu_" + s, (idx, t)))
                    if t == 0:
                        dve.wait_ge(*raise_of(b, "exp_bias_" + s, idx))
                    dve.scalar_tensor_tensor(g_row[s][:, t, :], g_row[s][:, t, :], slope, probs[s][:, t, :], ALU.mult, ALU.add)\
                       .then_inc(sig.raised("score_" + s, (idx, t)), 1)

            def one_over_sums(b, idx):
                s = leaky_of(idx)[0]
                dve.wait_ge(*raise_of(b, "probs_g_" + s, (idx, T - 1)))
                dve.reciprocal(row[s]["rden_g"][:], row[s]["sums_g"][:]).then_inc(sig.raised("rden_g_" + s, idx), 1)

            def front_stream(b):
                yield "h0"
                row_dots(b, 0)
                for half in range(2):
                    yield "g0", half
                    mask_rows(b, 0, half)
                for half in range(2):
                    yield "score0", half
                    score_rows(b, 0, half)
                yield "p0"
                dve.tensor_tensor(xa[:, :, H0:F], vals_a[:, :, 0:H0], xa[:, :, H0:F], ALU.add)\
                   .then_inc(sig.raised("y0", 0), 1)
                yield "a0"
                one_over_sums(b, 0)
                dve.wait_ge(*product_of(b, "a0"))
                dve.wait_ge(*raise_of(b, "rden_g_a", 0))
                for t in range(T):
                    sem = emptied("a0") if t == T - 1 else sig.raised("y0", 1 + t)
                    dve.scalar_tensor_tensor(xa[:, t, 0:H0], bank("a0")[:, t * P:(t + 1) * P], row["a"]["rden_g"][:, t:t + 1],
                                             xa[:, t, 0:H0], ALU.mult, ALU.add).then_inc(sem, 1)
                yield "stats0"
                dve.wait_ge(*moved(b, "a0"))
                norm_stats(b, 0, "a", xa)
                yield "norm0"
                norm(b, 0, "a", xa, xa)

                yield "x1"
                for k in range(KF):
                    low(b, ("x", 1, k), xt_lo[:, k, :], xt_hi[:, k, :])
                yield "q0"
                low(b, "q0", qk["q_lo"], qk["q_hi"], bq_c[:, 0:1])
                low(b, "k0", qk["k_lo"], qk["k_hi"], bk_c[:, 0:1])
                yield "v"
                for j in range(2):
                    dve.wait_ge(*product_of(b, f"v{j}"))
                    dve.tensor_tensor(two(vals_a, j), bank2(f"v{j}"), row2("bv"), ALU.add).then_inc(emptied(f"v{j}"), 1)
                for g in range(G1):
                    if g:
                        yield f"q{g}"
                        low(b, f"q{g}", qk["q_lo"], qk["q_hi"], bq_c[:, g:g + 1])
                        low(b, f"k{g}", qk["k_lo"], qk["k_hi"], bk_c[:, g:g + 1])
                    yield "stack", g
                    for hh in range(HG):
                        key = ("stack", g, "k", hh)
                        dve.wait_ge(*product_of(b, ("stack", g, "k", HG - 1) if hh >= 2 else key))
                        dve.tensor_copy(k_st[:, hh, :], bank(key)[:]).then_inc(emptied(key), 1)
                    for n in range(UNITS + LEAD):
                        yield "unit", g, n
                        if n < UNITS:
                            key = ("s", g, n)
                            dve.wait_ge(*product_of(b, key))
                            if n >= T or g:
                                before = (g, n - T) if n >= T else (g - 1, n + UNITS - T)
                                dve.wait_ge(*raise_of(b, "probs1", before))
                            settled()
                            dve.tensor_tensor_reduce(masked[:, n % T, :], bank(key)[:], edge_bias[:, n // HG, :], -SCALE1,
                                                     START_MIN, ALU.add, ALU.min,
                                                     neg_max[:, g * UNITS + n:g * UNITS + n + 1]).then_inc(emptied(key), 1)
                    yield "o", g
                    sums_of, rden_of = (m[:, :, g * HG:(g + 1) * HG] for m in (sums, rden))
                    dve.wait_ge(*raise_of(b, "probs1", (g, UNITS - 1)))
                    dve.tensor_tensor(rden_of, sums_of, has_edge[:].unsqueeze(2).to_broadcast([P, T, HG]), ALU.mult)\
                       .then_inc(sig.raised("sums1", g), 1)
                    dve.wait_ge(*raise_of(b, "sums1", g))
                    dve.reciprocal(rden_of, rden_of).then_inc(sig.raised("rden1", g), 1)
                    yield "r", g
                    dve.wait_ge(*product_of(b, f"r{g}"))
                    for bank_i in range(FB):
                        keys = [("o", g, t) for t in range(T) if place["o", g, t] == bank_i != place[f"r{g}"]]
                        if keys:
                            dve.wait_ge(*moved(b, keys[-1]))
                    dve.tensor_tensor(o_t[:, g, :], bank(f"r{g}")[:], o_t[:, g, :], ALU.mult).then_inc(emptied(f"r{g}"), 1)
                for j in range(2):
                    yield "w", j
                    if j == 0:
                        dve.wait_ge(*raise_of(b, "with_bo", 1))
                    key = f"w{j}"
                    dve.wait_ge(*product_of(b, key))
                    dve.tensor_tensor(two(xa, j), bank2(key), two(xa, j), ALU.add).then_inc(emptied(key), 1)
                yield "stats1"
                for j in range(2):
                    dve.wait_ge(*moved(b, f"w{j}"))
                norm_stats(b, 1, "a", xa)
                yield "norm1"
                norm(b, 1, "a", xa, xa)

                yield "x2"
                for k in range(KF):
                    low(b, ("x", 2, k), xt_lo[:, k, :], xt_hi[:, k, :])
                yield "mj"
                for j in range(2):
                    low(b, f"mj{j}", flat2(m_lo, j), flat2(m_hi, j))
                yield "mi"
                dve.wait_ge(*raise_of(b, "with_b2", 1))
                for t in range(T):
                    key = f"mi{t // 2}"
                    if t % 2 == 0:
                        dve.wait_ge(*product_of(b, key))
                    dve.scalar_tensor_tensor(sums3[:, t, :], bank2(key)[:, t % 2, :], degree[:, t:t + 1], xa[:, t, :],
                                             ALU.mult, ALU.add).then_inc(emptied(key) if t % 2 else sig.raised("y2", t), 1)
                yield "am"
                for j in range(2):
                    dve.wait_ge(*moved(b, f"mi{j}"))
                for j in range(2):
                    key = ("am", j)
                    dve.wait_ge(*product_of(b, key))
                    dve.tensor_tensor(two(sums3, j), bank2(key), two(sums3, j), ALU.add).then_inc(emptied(key), 1)
                yield "stats2"
                for j in range(2):
                    dve.wait_ge(*moved(b, ("am", j)))
                norm_stats(b, 2, "a", sums3)
                yield "norm2"
                if not isinstance(b, int):
                    dve.wait_ge(*raise_of(b - 1, "y4", T - 1))
                norm(b, 2, "a", sums3, xb)

            def back_stream(b):
                yield "x3"
                for k in range(KF):
                    low(b, ("x", 3, k), xu_lo[:, k, :], xu_hi[:, k, :])
                yield "wh", 0
                row_dots(b, 1)
                for half in range(2):
                    yield "g3", 0, half
                    mask_rows(b, 1, half)
                for half in range(2):
                    yield "score3", 0, half
                    score_rows(b, 1, half)
                for h in range(H3 + 1):
                    yield "p3", h
                    one_over_sums(b, 1 + h)
                    if h + 1 < H3:
                        yield "wh", h + 1
                        row_dots(b, 2 + h)
                        for half in range(2):
                            yield "g3", h + 1, half
                            mask_rows(b, 2 + h, half)
                    for j in range(2):
                        yield "a3", h, j
                        key = ("a3", h, j)
                        dve.wait_ge(*raise_of(b, "elu_exp", (h, 2 * j + 1)))
                        dve.tensor_scalar(flat2(h_sb, j), flat2(h_sb, j), 1.0, -1.0, ALU.min, ALU.add)\
                           .then_inc(sig.raised("elm", (h, j)), 1)
                        dve.wait_ge(*raise_of(b, "elm", (h, j)))
                        for i in range(2):
                            t = 2 * j + i
                            sem = emptied(key) if i else sig.raised("elu", (h, j))
                            dve.scalar_tensor_tensor(h_sb[:, t, :], bank2(key)[:, i, :], row["b"]["rden_g"][:, t:t + 1],
                                                     h_sb[:, t, :], ALU.mult, ALU.max).then_inc(sem, 1)
                    if h + 1 < H3:
                        for half in range(2):
                            yield "score3", h + 1, half
                            score_rows(b, 2 + h, half)
                    if h == H3 - 1:
                        yield "values", H3
                        row_dots(b, 1 + H3)
                        for half in range(2):
                            yield "g3", H3, half
                            mask_rows(b, 1 + H3, half)
                        for half in range(2):
                            yield "score3", H3, half
                            score_rows(b, 1 + H3, half)
                for j in range(2):
                    yield "e", j
                    if j == 0:
                        dve.wait_ge(*raise_of(b, "with_fb2", 1))
                    key = f"e{j}"
                    dve.wait_ge(*product_of(b, key))
                    dve.tensor_tensor(two(h_sb, j), bank2(key), two(h_sb, j), ALU.add).then_inc(emptied(key), 1)
                yield "stats3"
                for j in range(2):
                    dve.wait_ge(*moved(b, f"e{j}"))
                norm_stats(b, 3, "b", h_sb)
                yield "norm3"
                for t in range(T):
                    dve.scalar_tensor_tensor(h_sb[:, t, :], h_sb[:, t, :], mv["b"][:, t, 0:1], rows["gamma"][:], ALU.subtract,
                                             ALU.mult).then_inc(sig.raised("scaled", t), 1)
                dve.wait_ge(*raise_of(b, "with_beta", 1))
                for t in range(T):
                    dve.wait_ge(*raise_of(b, "scaled", t))
                    if t == 0:
                        dve.wait_ge(*raise_of(b, "rstd_b", 3))
                    dve.scalar_tensor_tensor(h_sb[:, t, :], h_sb[:, t, :], row["b"]["rstd"][:, t:t + 1], xb[:, t, :], ALU.mult,
                                             ALU.add).then_inc(sig.raised("y4", t), 1)
                yield "stats4"
                dve.wait_ge(*raise_of(b, "y4", T - 1))
                norm_stats(b, 4, "b", h_sb)
                yield "norm4"
                norm(b, 4, "b", h_sb, h_sb)

            both(front_stream, back_stream, dve.Fori)
    return sig.seen


_INS = ['x', 'adj', 'adj_t', 'L0_gnn_W', 'L0_gnn_a', 'wq_t', 'L1_gnn_bq', 'wk_t', 'L1_gnn_bk', 'wv_t', 'L1_gnn_bv', 'wo_t',
        'L1_gnn_bo', 'w2_t', 'L2_gnn_b', 'L3_gnn_W_heads', 'L3_gnn_a_heads', 'L3_gnn_W_out', 'L3_gnn_a_out', 'L3_gnn_w1',
        'L3_gnn_b1', 'L3_gnn_w2', 'L3_gnn_b2', 'L3_gnn_ln_gamma', 'L3_gnn_ln_beta']


def kernel(**inputs):
    import numpy as _np
    import concourse.bacc as _bacc
    from concourse import mybir as _mybir
    from concourse.bass_utils import run_bass_kernel_spmd as _run

    given = {k: _np.asarray(v) for k, v in inputs.items()}
    for name, src in (("wq_t", "L1_gnn_Wq"), ("wk_t", "L1_gnn_Wk"), ("wv_t", "L1_gnn_Wv"), ("wo_t", "L1_gnn_Wo"),
                      ("adj_t", "adj")):
        given[name] = _np.ascontiguousarray(given[src].T)
    w2 = given["L2_gnn_W"]
    half = w2.shape[1] // 2
    given["w2_t"] = _np.ascontiguousarray(_np.concatenate([w2[:, :half].T, w2[:, half:].T], axis=1))

    def program(order):
        nc = _bacc.Bacc("TRN2", target_bir_lowering=False, num_devices=1)
        arrays, args = {}, []
        for name in _INS:
            a = _np.ascontiguousarray(given[name])
            arrays[f"in_{name}"] = a
            args.append(nc.dram_tensor(f"in_{name}", a.shape, _mybir.dt.from_np(a.dtype), kind="ExternalInput").ap())
        args.append(nc.dram_tensor("out_0", given["x"].shape, _mybir.dt.float32, kind="ExternalOutput").ap())
        return nc, arrays, gat_mix_program(nc, *args, order)

    _, _, order = program({})
    nc, arrays, _ = program(order)
    r = _run(nc, [arrays], core_ids=[0])
    return r.results[0]["out_0"]
```
